# Optimizing a Trainium2 kernel written in Bass

```python
import numpy as np
import jax
import jax.numpy as jnp

def _softmax(x, axis=-1):
    return jax.nn.softmax(x, axis=axis)
def _gelu(x):
    return jax.nn.gelu(x, approximate=True)
def _silu(x):
    return jax.nn.silu(x)
def _sigmoid(x):
    return jax.nn.sigmoid(x)
def _layernorm(x, axis=-1, eps=1e-5):
    m = jnp.mean(x, axis=axis, keepdims=True)
    v = jnp.var(x, axis=axis, keepdims=True)
    return (x - m) / jnp.sqrt(v + eps)
def _scatter_add(tgt, idx, src, axis=0):
    return tgt.at[idx].add(src)
def _segment_sum(src, seg, n):
    return jax.ops.segment_sum(src, seg, n)

kernel_name = 'mk_adj_ffn_d2_adj_256_940ede'

def setup_inputs(seed: int = 0):
    np.random.seed(seed)
    _w = jnp.asarray
    def _rec_inputs():
        import jax
        import jax.numpy as jnp
        _gk = jax.random.key(seed)
        x = -0.0005207 + 1.001 * jax.random.normal(jax.random.fold_in(_gk, 1), (3327, 256), jnp.float32)
        _w = (1.0 + jnp.arange(3327, dtype=jnp.float32)) ** -0.5
        _w = _w / _w.mean()
        _pij = jnp.clip(0.00480914 * _w[:, None] * _w[None, :], 0.0, 1.0)
        _a = jax.random.uniform(jax.random.fold_in(_gk, 2), (3327, 3327)) < _pij
        _a = jnp.logical_or(_a, jnp.eye(3327, dtype=bool))
        _af = _a.astype(jnp.float32)
        _af = _af * jax.random.uniform(jax.random.fold_in(_gk, 3), (3327, 3327), jnp.float32, 0.05, 1)
        adj = _af
        return x, adj
    x, adj = _rec_inputs()
    def _L0_gnn_setup():
        import jax, jax.numpy as jnp
        import numpy as np
        N = 8192
        F_IN = 256
        F_OUT = 256
        key = jax.random.key(seed)
        k1, k2, k3, k4 = jax.random.split(key, 4)
        x = jax.random.normal(k1, (N, F_IN), dtype=jnp.float32)
        adj = jax.random.uniform(k2, (N, N), dtype=jnp.float32)
        bound = 1.0 / np.sqrt(F_IN)
        W = jax.random.uniform(k3, (F_OUT, F_IN), dtype=jnp.float32, minval=-bound, maxval=bound)
        b = jax.random.uniform(k4, (F_OUT,), dtype=jnp.float32, minval=-bound, maxval=bound)
        return {'x': x, 'adj': adj, 'W': W, 'b': b}
    _L0_gnn_all = _L0_gnn_setup()
    _L0_gnn_in = {k: v for k, v in _L0_gnn_all.items() if k in ('W', 'b', )}
    del _L0_gnn_all

    def _L0_ffn_setup():
        import jax, jax.numpy as jnp
        import numpy as np
        H, P, G, NS, K = (8, 64, 64, 64, 3)
        D_INNER = H * P
        CONV_DIM = D_INNER + 2 * NS
        D_IN_PROJ = 2 * D_INNER + 2 * NS + 2 * H

        def _hydra(u, in_w, conv_w, conv_b, dt_bias, A_log, Dp, fcD_w, norm_w, out_w):
            Bt, L, _ = u.shape
            zxbcdt = u @ in_w.T
            z = zxbcdt[..., :D_INNER]
            xBC = zxbcdt[..., D_INNER:D_INNER + CONV_DIM]
            dt = zxbcdt[..., -2 * H:]
            dt = jnp.concatenate([dt[..., :H], jnp.flip(dt[..., H:], axis=1)], axis=0)
            dt = jax.nn.softplus(dt + dt_bias)
            xp = jnp.pad(xBC, ((0, 0), (K - 1, 0), (0, 0)))
            xBC = sum((xp[:, k:k + L, :] * conv_w[:, k] for k in range(K))) + conv_b
            xBC = jax.nn.silu(xBC)
            x = xBC[..., :D_INNER]
            Bm = xBC[..., D_INNER:D_INNER + NS]
            Cm = xBC[..., D_INNER + NS:]
            x_og = x
            x2 = jnp.concatenate([x, jnp.flip(x, 1)], 0).reshape(2 * Bt, L, H, P)
            B2 = jnp.concatenate([Bm, jnp.flip(Bm, 1)], 0)
            C2 = jnp.concatenate([Cm, jnp.flip(Cm, 1)], 0)
            dA = jnp.exp(dt * -jnp.exp(A_log))
            dBx = jnp.einsum('blh,bln,blhp->blhpn', dt, B2, x2)

            def step(h, inp):
                dA_t, dBx_t, C_t = inp
                h = h * dA_t[:, :, None, None] + dBx_t
                return (h, jnp.einsum('bhpn,bn->bhp', h, C_t))
            h0 = jnp.zeros((2 * Bt, H, P, NS), u.dtype)
            _, ys = jax.lax.scan(step, h0, (dA.transpose(1, 0, 2), dBx.transpose(1, 0, 2, 3, 4), C2.transpose(1, 0, 2)))
            y = ys.transpose(1, 0, 2, 3).reshape(2 * Bt, L, D_INNER)
            y_fw, y_bw = (y[:Bt], jnp.flip(y[Bt:], 1))
            y = jnp.pad(y_fw[:, :-1], ((0, 0), (1, 0), (0, 0))) + jnp.pad(y_bw[:, 1:], ((0, 0), (0, 1), (0, 0)))
            y = y + x_og * jnp.repeat(x_og @ fcD_w.T + Dp, P, axis=-1)
            yg = y * jax.nn.silu(z)
            yg = yg * jax.lax.rsqrt(jnp.mean(jnp.square(yg), -1, keepdims=True) + 1e-05) * norm_w
            return yg @ out_w.T
        key = jax.random.key(seed)
        ks = jax.random.split(key, 10)
        dim, Bsz, N = (256, 4, 8192)
        s = 0.02
        return {'x': jax.random.normal(ks[0], (Bsz, N, dim), jnp.float32), 'W_fx': jax.random.normal(ks[1], (D_INNER, dim), jnp.float32) * s, 'b_fx': jnp.zeros((D_INNER,), jnp.float32), 'W_x': jax.random.normal(ks[2], (D_INNER, dim), jnp.float32) * s, 'b_x': jnp.zeros((D_INNER,), jnp.float32), 'W_slice': jax.random.normal(ks[3], (G, P), jnp.float32) * s, 'b_slice': jnp.zeros((G,), jnp.float32), 'temperature': jnp.full((1, H, 1, 1), 0.5, jnp.float32), 'hy_in_w': jax.random.normal(ks[4], (D_IN_PROJ, D_INNER), jnp.float32) * s, 'hy_conv_w': jax.random.normal(ks[5], (CONV_DIM, K), jnp.float32) * s, 'hy_conv_b': jnp.zeros((CONV_DIM,), jnp.float32), 'hy_dt_bias': jnp.log(jnp.expm1(jnp.full((H,), 0.01, jnp.float32))), 'hy_A_log': jnp.log(jnp.linspace(1.0, 16.0, H)).astype(jnp.float32), 'hy_D': jnp.ones((H,), jnp.float32), 'hy_fcD_w': jax.random.normal(ks[6], (H, D_INNER), jnp.float32) * s, 'hy_norm_w': jnp.ones((D_INNER,), jnp.float32), 'hy_out_w': jax.random.normal(ks[7], (D_INNER, D_INNER), jnp.float32) * s, 'out_w': jax.random.normal(ks[8], (dim, D_INNER), jnp.float32) * s, 'out_b': jnp.zeros((dim,), jnp.float32)}
    _L0_ffn_all = _L0_ffn_setup()
    _L0_ffn_in = {k: v for k, v in _L0_ffn_all.items() if k in ('W_fx', 'b_fx', 'W_x', 'b_x', 'W_slice', 'b_slice', 'temperature', 'hy_in_w', 'hy_conv_w', 'hy_conv_b', 'hy_dt_bias', 'hy_A_log', 'hy_D', 'hy_fcD_w', 'hy_norm_w', 'hy_out_w', 'out_w', 'out_b', )}
    del _L0_ffn_all

    def _L1_gnn_setup():
        import jax, jax.numpy as jnp
        import numpy as np
        N = 8192
        IN_CH = 256
        HEADS = 8
        OUT_CH = 32
        HID = HEADS * OUT_CH
        NEG_SLOPE = 0.2
        MASK_VAL = -1000000000.0
        EDGE_PROB = 0.06
        key = jax.random.key(seed)
        k_nodes, k_adj, k_w, k_c1, k_c2 = jax.random.split(key, 5)
        nodes = jax.random.normal(k_nodes, (N, IN_CH), dtype=jnp.float32)
        u = jax.random.uniform(k_adj, (N, N), dtype=jnp.float32)
        adj_bias_mat = jnp.where(u < EDGE_PROB, 0.0, MASK_VAL).astype(jnp.float32)
        adj_bias_mat = adj_bias_mat.at[jnp.arange(N), jnp.arange(N)].set(0.0)
        weight = jax.random.normal(k_w, (IN_CH, HID), dtype=jnp.float32) * np.sqrt(2.0 / (IN_CH + HID))
        conv_weight1 = jax.random.normal(k_c1, (HID, 1), dtype=jnp.float32) * np.sqrt(2.0 / (HID + 1))
        conv_weight2 = jax.random.normal(k_c2, (HID, 1), dtype=jnp.float32) * np.sqrt(2.0 / (HID + 1))
        bias = jnp.zeros((HID,), dtype=jnp.float32)
        return {'nodes': nodes, 'adj_bias_mat': adj_bias_mat, 'weight': weight, 'conv_weight1': conv_weight1, 'conv_weight2': conv_weight2, 'bias': bias}
    _L1_gnn_all = _L1_gnn_setup()
    _L1_gnn_in = {k: v for k, v in _L1_gnn_all.items() if k in ('weight', 'conv_weight1', 'conv_weight2', 'bias', )}
    del _L1_gnn_all

    def _L1_ffn_setup():
        import jax, jax.numpy as jnp
        import numpy as np
        B, S, H, NH, NE = (4, 1024, 256, 4, 4)
        D = H // NH
        EPS = 1e-08

        def layernorm(x, g, b):
            m = jnp.mean(x, axis=-1, keepdims=True)
            v = jnp.mean((x - m) ** 2, axis=-1, keepdims=True)
            return (x - m) / jnp.sqrt(v + EPS) * g + b
        key = jax.random.key(seed)
        ks = jax.random.split(key, 18)
        sc = 0.05
        return {'x': jax.random.normal(ks[0], (B, S, H), jnp.float32), 'hl_w': jax.random.normal(ks[1], (NH, D, H), jnp.float32) * sc, 'hl_b': jax.random.normal(ks[2], (NH, D), jnp.float32) * sc, 'wq': jax.random.normal(ks[3], (NH, NE, D, D), jnp.float32) * sc, 'wk': jax.random.normal(ks[4], (NH, D, D), jnp.float32) * sc, 'wv': jax.random.normal(ks[5], (NH, D, D), jnp.float32) * sc, 'gate_w': jax.random.normal(ks[6], (NH, NE, NE * D), jnp.float32) * sc, 'gate_b': jax.random.normal(ks[7], (NH, NE), jnp.float32) * sc, 'ln_g': jnp.ones((D,), jnp.float32), 'ln_b': jnp.zeros((D,), jnp.float32), 'fc1_w': jax.random.normal(ks[8], (D, D), jnp.float32) * sc, 'fc1_b': jax.random.normal(ks[9], (D,), jnp.float32) * sc, 'fc2_w': jax.random.normal(ks[10], (D, D), jnp.float32) * sc, 'fc2_b': jax.random.normal(ks[11], (D,), jnp.float32) * sc, 'fnorm_g': jnp.ones((D,), jnp.float32), 'fnorm_b': jnp.zeros((D,), jnp.float32), 'fgate_w': jax.random.normal(ks[12], (NH, H), jnp.float32) * sc}
    _L1_ffn_all = _L1_ffn_setup()
    _L1_ffn_in = {k: v for k, v in _L1_ffn_all.items() if k in ('hl_w', 'hl_b', 'wq', 'wk', 'wv', 'gate_w', 'gate_b', 'ln_g', 'ln_b', 'fc1_w', 'fc1_b', 'fc2_w', 'fc2_b', 'fnorm_g', 'fnorm_b', 'fgate_w', )}
    del _L1_ffn_all

    return {
        "x": x,
        "adj": adj,
        "L0_gnn_W": _L0_gnn_in["W"],
        "L0_gnn_b": _L0_gnn_in["b"],
        "L0_ffn_W_fx": _L0_ffn_in["W_fx"],
        "L0_ffn_b_fx": _L0_ffn_in["b_fx"],
        "L0_ffn_W_x": _L0_ffn_in["W_x"],
        "L0_ffn_b_x": _L0_ffn_in["b_x"],
        "L0_ffn_W_slice": _L0_ffn_in["W_slice"],
        "L0_ffn_b_slice": _L0_ffn_in["b_slice"],
        "L0_ffn_temperature": _L0_ffn_in["temperature"],
        "L0_ffn_hy_in_w": _L0_ffn_in["hy_in_w"],
        "L0_ffn_hy_conv_w": _L0_ffn_in["hy_conv_w"],
        "L0_ffn_hy_conv_b": _L0_ffn_in["hy_conv_b"],
        "L0_ffn_hy_dt_bias": _L0_ffn_in["hy_dt_bias"],
        "L0_ffn_hy_A_log": _L0_ffn_in["hy_A_log"],
        "L0_ffn_hy_D": _L0_ffn_in["hy_D"],
        "L0_ffn_hy_fcD_w": _L0_ffn_in["hy_fcD_w"],
        "L0_ffn_hy_norm_w": _L0_ffn_in["hy_norm_w"],
        "L0_ffn_hy_out_w": _L0_ffn_in["hy_out_w"],
        "L0_ffn_out_w": _L0_ffn_in["out_w"],
        "L0_ffn_out_b": _L0_ffn_in["out_b"],
        "L1_gnn_weight": _L1_gnn_in["weight"],
        "L1_gnn_conv_weight1": _L1_gnn_in["conv_weight1"],
        "L1_gnn_conv_weight2": _L1_gnn_in["conv_weight2"],
        "L1_gnn_bias": _L1_gnn_in["bias"],
        "L1_ffn_hl_w": _L1_ffn_in["hl_w"],
        "L1_ffn_hl_b": _L1_ffn_in["hl_b"],
        "L1_ffn_wq": _L1_ffn_in["wq"],
        "L1_ffn_wk": _L1_ffn_in["wk"],
        "L1_ffn_wv": _L1_ffn_in["wv"],
        "L1_ffn_gate_w": _L1_ffn_in["gate_w"],
        "L1_ffn_gate_b": _L1_ffn_in["gate_b"],
        "L1_ffn_ln_g": _L1_ffn_in["ln_g"],
        "L1_ffn_ln_b": _L1_ffn_in["ln_b"],
        "L1_ffn_fc1_w": _L1_ffn_in["fc1_w"],
        "L1_ffn_fc1_b": _L1_ffn_in["fc1_b"],
        "L1_ffn_fc2_w": _L1_ffn_in["fc2_w"],
        "L1_ffn_fc2_b": _L1_ffn_in["fc2_b"],
        "L1_ffn_fnorm_g": _L1_ffn_in["fnorm_g"],
        "L1_ffn_fnorm_b": _L1_ffn_in["fnorm_b"],
        "L1_ffn_fgate_w": _L1_ffn_in["fgate_w"],
    }

def reference(x, adj, L0_gnn_W, L0_gnn_b, L0_ffn_W_fx, L0_ffn_b_fx, L0_ffn_W_x, L0_ffn_b_x, L0_ffn_W_slice, L0_ffn_b_slice, L0_ffn_temperature, L0_ffn_hy_in_w, L0_ffn_hy_conv_w, L0_ffn_hy_conv_b, L0_ffn_hy_dt_bias, L0_ffn_hy_A_log, L0_ffn_hy_D, L0_ffn_hy_fcD_w, L0_ffn_hy_norm_w, L0_ffn_hy_out_w, L0_ffn_out_w, L0_ffn_out_b, L1_gnn_weight, L1_gnn_conv_weight1, L1_gnn_conv_weight2, L1_gnn_bias, L1_ffn_hl_w, L1_ffn_hl_b, L1_ffn_wq, L1_ffn_wk, L1_ffn_wv, L1_ffn_gate_w, L1_ffn_gate_b, L1_ffn_ln_g, L1_ffn_ln_b, L1_ffn_fc1_w, L1_ffn_fc1_b, L1_ffn_fc2_w, L1_ffn_fc2_b, L1_ffn_fnorm_g, L1_ffn_fnorm_b, L1_ffn_fgate_w):
    import jax
    import jax.numpy as jnp
    def _L0_gnn_ref(x, adj, W, b):
        import jax, jax.numpy as jnp
        import numpy as np
        N = 8192
        F_IN = 256
        F_OUT = 256
        D = jnp.sum(adj, axis=1)
        d_inv_sqrt = jnp.power(D + 1e-09, -0.5)
        adj_norm = adj * d_inv_sqrt[:, None] * d_inv_sqrt[None, :]
        h = adj_norm @ x
        out = h @ W.T + b
        return jax.nn.relu(out)

    def _L0_ffn_ref(x, W_fx, b_fx, W_x, b_x, W_slice, b_slice, temperature, hy_in_w, hy_conv_w, hy_conv_b, hy_dt_bias, hy_A_log, hy_D, hy_fcD_w, hy_norm_w, hy_out_w, out_w, out_b):
        import jax, jax.numpy as jnp
        import numpy as np
        H, P, G, NS, K = (8, 64, 64, 64, 3)
        D_INNER = H * P
        CONV_DIM = D_INNER + 2 * NS
        D_IN_PROJ = 2 * D_INNER + 2 * NS + 2 * H

        def _hydra(u, in_w, conv_w, conv_b, dt_bias, A_log, Dp, fcD_w, norm_w, out_w):
            Bt, L, _ = u.shape
            zxbcdt = u @ in_w.T
            z = zxbcdt[..., :D_INNER]
            xBC = zxbcdt[..., D_INNER:D_INNER + CONV_DIM]
            dt = zxbcdt[..., -2 * H:]
            dt = jnp.concatenate([dt[..., :H], jnp.flip(dt[..., H:], axis=1)], axis=0)
            dt = jax.nn.softplus(dt + dt_bias)
            xp = jnp.pad(xBC, ((0, 0), (K - 1, 0), (0, 0)))
            xBC = sum((xp[:, k:k + L, :] * conv_w[:, k] for k in range(K))) + conv_b
            xBC = jax.nn.silu(xBC)
            x = xBC[..., :D_INNER]
            Bm = xBC[..., D_INNER:D_INNER + NS]
            Cm = xBC[..., D_INNER + NS:]
            x_og = x
            x2 = jnp.concatenate([x, jnp.flip(x, 1)], 0).reshape(2 * Bt, L, H, P)
            B2 = jnp.concatenate([Bm, jnp.flip(Bm, 1)], 0)
            C2 = jnp.concatenate([Cm, jnp.flip(Cm, 1)], 0)
            dA = jnp.exp(dt * -jnp.exp(A_log))
            dBx = jnp.einsum('blh,bln,blhp->blhpn', dt, B2, x2)

            def step(h, inp):
                dA_t, dBx_t, C_t = inp
                h = h * dA_t[:, :, None, None] + dBx_t
                return (h, jnp.einsum('bhpn,bn->bhp', h, C_t))
            h0 = jnp.zeros((2 * Bt, H, P, NS), u.dtype)
            _, ys = jax.lax.scan(step, h0, (dA.transpose(1, 0, 2), dBx.transpose(1, 0, 2, 3, 4), C2.transpose(1, 0, 2)))
            y = ys.transpose(1, 0, 2, 3).reshape(2 * Bt, L, D_INNER)
            y_fw, y_bw = (y[:Bt], jnp.flip(y[Bt:], 1))
            y = jnp.pad(y_fw[:, :-1], ((0, 0), (1, 0), (0, 0))) + jnp.pad(y_bw[:, 1:], ((0, 0), (0, 1), (0, 0)))
            y = y + x_og * jnp.repeat(x_og @ fcD_w.T + Dp, P, axis=-1)
            yg = y * jax.nn.silu(z)
            yg = yg * jax.lax.rsqrt(jnp.mean(jnp.square(yg), -1, keepdims=True) + 1e-05) * norm_w
            return yg @ out_w.T
        B, N, _ = x.shape
        fx = (x @ W_fx.T + b_fx).reshape(B, N, H, P).transpose(0, 2, 1, 3)
        xm = (x @ W_x.T + b_x).reshape(B, N, H, P).transpose(0, 2, 1, 3)
        temp = jnp.maximum(temperature, 1e-06)
        sw = jax.nn.softmax((xm @ W_slice.T + b_slice) / temp, axis=-1)
        snorm = sw.sum(2)
        st = jnp.einsum('bhnc,bhng->bhgc', fx, sw) / (snorm + 1e-05)[..., None]
        st = st.transpose(0, 2, 1, 3).reshape(B, G, D_INNER)
        ot = _hydra(st, hy_in_w, hy_conv_w, hy_conv_b, hy_dt_bias, hy_A_log, hy_D, hy_fcD_w, hy_norm_w, hy_out_w)
        ot = ot.reshape(B, G, H, P).transpose(0, 2, 1, 3)
        out = jnp.einsum('bhgc,bhng->bhnc', ot, sw).transpose(0, 2, 1, 3).reshape(B, N, D_INNER)
        return out @ out_w.T + out_b

    def _L1_gnn_ref(nodes, adj_bias_mat, weight, conv_weight1, conv_weight2, bias):
        import jax, jax.numpy as jnp
        import numpy as np
        N = 8192
        IN_CH = 256
        HEADS = 8
        OUT_CH = 32
        HID = HEADS * OUT_CH
        NEG_SLOPE = 0.2
        MASK_VAL = -1000000000.0
        EDGE_PROB = 0.06
        h = nodes @ weight
        f1 = h @ conv_weight1
        f2 = h @ conv_weight2
        logits = f1 + f2.T
        coefs = jax.nn.softmax(jax.nn.leaky_relu(logits, negative_slope=NEG_SLOPE) + adj_bias_mat, axis=-1)
        vals = coefs @ h + bias
        return vals

    def _L1_ffn_ref(x, hl_w, hl_b, wq, wk, wv, gate_w, gate_b, ln_g, ln_b, fc1_w, fc1_b, fc2_w, fc2_b, fnorm_g, fnorm_b, fgate_w):
        import jax, jax.numpy as jnp
        import numpy as np
        B, S, H, NH, NE = (4, 1024, 256, 4, 4)
        D = H // NH
        EPS = 1e-08

        def layernorm(x, g, b):
            m = jnp.mean(x, axis=-1, keepdims=True)
            v = jnp.mean((x - m) ** 2, axis=-1, keepdims=True)
            return (x - m) / jnp.sqrt(v + EPS) * g + b
        b, s, h = x.shape
        nh, d, _ = wk.shape
        ne = wq.shape[1]
        sx = jnp.einsum('bsh,ndh->bnsd', x, hl_w) + hl_b[None, :, None, :]
        pad = sx == 0
        q = jnp.einsum('bnsd,neod->bneso', sx, wq)
        k = jnp.einsum('bnsd,nod->bnso', sx, wk)
        v = jnp.einsum('bnsd,nod->bnso', sx, wv)
        causal = jnp.where(jnp.tril(jnp.ones((s, s), bool)), 0.0, -jnp.inf).astype(x.dtype)
        scores = jnp.einsum('bnesd,bntd->bnest', q, k) * d ** 0.5 + causal
        att = jax.nn.softmax(scores, axis=-1)
        qkv = jnp.einsum('bnest,bntd->bnesd', att, v)
        qkv = jnp.where(pad[:, :, None], 0.0, qkv)
        out = jnp.transpose(qkv, (0, 1, 3, 2, 4)).reshape(b, nh, s, ne * d)
        gs = jax.nn.softmax(jnp.einsum('bnsf,nef->bnse', out, gate_w) + gate_b[None, :, None, :], axis=-1)
        mixed = jnp.einsum('bnsed,bnse->bnsd', out.reshape(b, nh, s, ne, d), gs)
        resid = sx[jnp.arange(nh), jnp.arange(nh)]
        hn = layernorm(mixed + resid, ln_g, ln_b)
        f_n = jnp.transpose(hn, (0, 2, 1, 3)).reshape(b, s, h)
        fx = f_n.reshape(b, s, nh, d)
        pm = fx == 0
        hx = jnp.where(pm, 0.0, fx @ fc1_w.T + fc1_b)
        hx = jax.nn.relu(hx)
        hx = jnp.where(pm, 0.0, hx @ fc2_w.T + fc2_b)
        hx = layernorm(hx + fx, fnorm_g, fnorm_b)
        fout = hx.reshape(b, s, h)
        fg = jax.nn.softmax(fout @ fgate_w.T, axis=-1)
        return (fout.reshape(b, s, nh, d) * fg[..., None]).reshape(b, s, h)

    x = x + _L0_gnn_ref(_layernorm(x, axis=-1), adj, L0_gnn_W, L0_gnn_b)
    x = x + _L0_ffn_ref((_layernorm(x, axis=-1))[None], L0_ffn_W_fx, L0_ffn_b_fx, L0_ffn_W_x, L0_ffn_b_x, L0_ffn_W_slice, L0_ffn_b_slice, L0_ffn_temperature, L0_ffn_hy_in_w, L0_ffn_hy_conv_w, L0_ffn_hy_conv_b, L0_ffn_hy_dt_bias, L0_ffn_hy_A_log, L0_ffn_hy_D, L0_ffn_hy_fcD_w, L0_ffn_hy_norm_w, L0_ffn_hy_out_w, L0_ffn_out_w, L0_ffn_out_b)[0]
    x = x + _L1_gnn_ref(_layernorm(x, axis=-1), adj, L1_gnn_weight, L1_gnn_conv_weight1, L1_gnn_conv_weight2, L1_gnn_bias)
    x = x + _L1_ffn_ref((_layernorm(x, axis=-1))[None], L1_ffn_hl_w, L1_ffn_hl_b, L1_ffn_wq, L1_ffn_wk, L1_ffn_wv, L1_ffn_gate_w, L1_ffn_gate_b, L1_ffn_ln_g, L1_ffn_ln_b, L1_ffn_fc1_w, L1_ffn_fc1_b, L1_ffn_fc2_w, L1_ffn_fc2_b, L1_ffn_fnorm_g, L1_ffn_fnorm_b, L1_ffn_fgate_w)[0]
    return x


_drawn_inputs = setup_inputs


def setup_inputs(seed=0):
    import zlib

    import numpy as np

    out = dict(_drawn_inputs(seed))
    spreads = {'L0_ffn_b_fx': (0.0, 0.1),
     'L0_ffn_b_x': (0.0, 0.8),
     'L0_ffn_b_slice': (0.0, 0.8),
     'L0_ffn_temperature': (0.5, 0.6),
     'L0_ffn_hy_conv_b': (0.0, 0.1),
     'L0_ffn_hy_dt_bias': (-4.600166320800781, 0.6),
     'L0_ffn_hy_D': (1.0, 0.6),
     'L0_ffn_hy_norm_w': (1.0, 0.6),
     'L0_ffn_out_b': (0.0, 0.1),
     'L1_gnn_bias': (0.0, 0.1),
     'L1_ffn_ln_g': (1.0, 0.2),
     'L1_ffn_ln_b': (0.0, 0.27),
     'L1_ffn_fnorm_g': (1.0, 0.2),
     'L1_ffn_fnorm_b': (0.0, 0.1)}
    factors = {'L0_ffn_W_fx': 6.136,
     'L0_ffn_W_x': 8.0,
     'L0_ffn_W_slice': 8.0,
     'L0_ffn_hy_conv_w': 8.0,
     'L0_ffn_hy_A_log': 8.0,
     'L0_ffn_hy_fcD_w': 8.0,
     'L1_ffn_gate_b': 8.0,
     'L1_ffn_fc1_b': 8.0,
     'L1_ffn_fc2_b': 3.687}
    for name, (base, spread) in spreads.items():
        noise = np.random.default_rng([zlib.crc32(name.encode()), seed]).standard_normal(out[name].shape)
        drawn = base * np.exp(spread * noise) if base else spread * noise
        out[name] = jnp.asarray(drawn.astype(out[name].dtype))
    for name, factor in factors.items():
        out[name] = (out[name] * factor).astype(out[name].dtype)
    return out
```

```python
from contextlib import ExitStack

import numpy as np

import concourse.bass as bass
from concourse import mybir

ALU = mybir.AluOpType
ACT = mybir.ActivationFunctionType
AX = mybir.AxisListType
F32 = mybir.dt.float32
F32R = mybir.dt.float32r
BF16 = mybir.dt.bfloat16

P = 128
N = 3327
NT = (N + P - 1) // P
NP = NT * P
LAST = N - (NT - 1) * P
DM = 256
DC = DM // P
BLK = 512
NB = NP // BLK
TAIL = NP - NB * BLK
SUB = BLK // P
H, G, PH = 8, 64, 64
HG = H * G
KC = HG // P
LN_EPS = 1e-5


class Linker:

    def __init__(self, eng, sem, start=0):
        self.eng, self.sem, self.n = eng, sem, start

    def __call__(self, ins):
        ins.then_inc(self.sem, 1)
        self.n += 1
        self.eng.wait_ge(self.sem, self.n)


def blocks_of_tokens():
    return [(b * BLK, BLK) for b in range(NB)] + [(NB * BLK, TAIL)]


class Mem:

    def __init__(self, nc, ctx):
        self.nc, self.ctx, self.sems = nc, ctx, []
        ctx.callback(self.clear)

    def clear(self):
        if self.sems:
            self.nc.clear_and_free_semaphores(self.sems)
            self.nc.all_engine_barrier()

    def sb(self, name, shape, dt=F32):
        return self.ctx.enter_context(self.nc.sbuf_tensor(name, shape, dt))

    def ps(self, name, shape, dt=F32):
        return self.ctx.enter_context(self.nc.psum_tensor(name, shape, dt))

    def sem(self, name):
        self.sems.append(self.nc.alloc_semaphore(name))
        return self.sems[-1]


class LayerNorm:

    def __init__(self, mem, tag, X, xn, xt, ident, ps):
        self.X, self.xn, self.xt, self.ident, self.ps = X, xn, xt, ident, ps
        self.stats = mem.sb(f"{tag}_stats", [P, NT, 6])
        self.mv = mem.sb(f"{tag}_mv", [P, NT, 2])
        self.std = mem.sb(f"{tag}_std", [P, NT])
        self.rstd = mem.sb(f"{tag}_rstd", [P, NT])
        self.var_ready = mem.sem(f"{tag}_var_ready")
        self.std_ready = mem.sem(f"{tag}_std_ready")
        self.xn_ready = mem.sem(f"{tag}_xn_ready")
        self.turned = mem.sem(f"{tag}_turned")
        self.xt_ready = mem.sem(f"{tag}_xt_ready")

    def vector(self, eng, link):
        for t in range(NT):
            ins = eng.bn_stats(self.stats[:, t, :], self.X[:, t, :])
        link(ins)
        for t in range(NT):
            ins = eng.bn_aggr(self.mv[:, t, :], self.stats[:, t, :])
        link(ins)
        eng.tensor_scalar(self.rstd[:, :], self.mv[:, :, 1], LN_EPS, None, ALU.add).then_inc(self.var_ready, 1)
        eng.wait_ge(self.std_ready, 1)
        link(eng.reciprocal(self.rstd[:, :], self.std[:, :]))
        for t in range(NT):
            eng.tensor_scalar(self.xn[:, t, 0:DM], self.X[:, t, :], self.mv[:, t, 0:1], self.rstd[:, t:t + 1],
                              ALU.subtract, ALU.mult).then_inc(self.xn_ready, 1)

    def scalar(self, eng):
        eng.wait_ge(self.var_ready, 1)
        eng.activation(self.std[:, :], self.rstd[:, :], ACT.Sqrt).then_inc(self.std_ready, 1)
        if self.xt is None:
            return
        n = 0
        for c0, w in blocks_of_tokens():
            for c in range(DC):
                eng.wait_ge(self.turned, n + 1)
                eng.activation(self.xt[:, c, c0:c0 + w], self.ps[:, n % 2, 0:w], ACT.Copy).then_inc(self.xt_ready, 1)
                n += 1

    def tensor(self, eng):
        if self.xt is None:
            return
        n = 0
        for c0, w in blocks_of_tokens():
            eng.wait_ge(self.xn_ready, (c0 + w) // P)
            for c in range(DC):
                if n >= 2:
                    eng.wait_ge(self.xt_ready, n - 1)
                for s in range(w // P):
                    ins = eng.transpose(self.ps[:, n % 2, s * P:(s + 1) * P],
                                        self.xn[:, c0 // P + s, c * P:(c + 1) * P], self.ident[:, :])
                ins.then_inc(self.turned, 1)
                n += 1


def load_tokens(eng, X, src, sem):
    eng.dma_start(X[:, 0:NT - 1, :], src[0:(NT - 1) * P, :].rearrange("(t p) d -> p t d", p=P)).then_inc(sem, 16)
    eng.dma_start(X[0:LAST, NT - 1, :], src[(NT - 1) * P:N, :]).then_inc(sem, 16)


def store_tokens(eng, dst, X, sem):
    eng.dma_start(dst[0:(NT - 1) * P, :].rearrange("(t p) d -> p t d", p=P), X[:, 0:NT - 1, :]).then_inc(sem, 16)
    eng.dma_start(dst[(NT - 1) * P:N, :], X[0:LAST, NT - 1, :]).then_inc(sem, 16)


def row_on_all(ap, parts=P):
    return ap.partition_broadcast(parts)


def stage_degrees(nc, X, xn, dinv, ident, x_in, adj):
    SLOTS, SPLIT = 4, 1792
    with ExitStack() as ctx:
        m = Mem(nc, ctx)
        rows = m.sb("deg_rows", [P, SLOTS, NP])
        junk = m.sb("deg_junk", [P, NP - SPLIT])
        part = m.sb("deg_part", [P, 2, NT])
        deg = m.sb("deg", [P, NT])
        dsq = m.sb("deg_sqrt", [P, NT])
        x_loaded = m.sem("x_loaded")
        x_zero = m.sem("x_zero")
        ident_ready = m.sem("ident_ready")
        rows_loaded = [m.sem(f"rows_loaded{k}") for k in range(SLOTS)]
        sum_v = m.sem("sum_v")
        sum_a = m.sem("sum_a")
        chain = m.sem("deg_chain")
        deg_ready = m.sem("deg_ready")
        dsq_ready = m.sem("dsq_ready")
        ln = LayerNorm(m, "ln0", X, xn, None, ident, None)
        NTF = NT // SLOTS

        def tile_src(t):
            return adj[bass.ds(t * P, P), :]

        with nc.Block() as block:
            @block.sync
            def _(sp):
                sp.wait_ge(x_zero, 1)
                load_tokens(sp, X, x_in, x_loaded)
                for k in range(SLOTS):
                    sp.dma_start(rows[:, k, :], tile_src(k)).then_inc(rows_loaded[k], 16)
                with sp.Fori(1, NTF) as i:
                    for k in range(SLOTS):
                        sp.wait_ge(sum_v, (i - 1) * SLOTS + k + 1)
                        sp.wait_ge(sum_a, (i - 1) * SLOTS + k + 1)
                        sp.dma_start(rows[:, k, :], tile_src(i * SLOTS + k)).then_inc(rows_loaded[k], 16)
                for t in range(NTF * SLOTS, NT):
                    sp.wait_ge(sum_v, t - SLOTS + 1)
                    sp.wait_ge(sum_a, t - SLOTS + 1)
                    sp.dma_start(rows[:, t % SLOTS, :], tile_src(t)).then_inc(rows_loaded[t % SLOTS], 16)

            @block.gpsimd
            def _(pool):
                pool.memset(X[:, NT - 1, :], 0.0).then_inc(x_zero, 1)
                pool.memset(ident[:, :], 0.0).then_inc(ident_ready, 1)
                pool.wait_ge(ident_ready, 1)
                pool.affine_select(out=ident[:, :], in_=ident[:, :], compare_op=ALU.not_equal, fill=1.0, base=0,
                                   pattern=[[-1, P]], channel_multiplier=1).then_inc(ident_ready, 1)

            @block.vector
            def _(dve):
                link = Linker(dve, chain)
                dve.wait_ge(x_loaded, 32)
                ln.vector(dve, link)

                def half_sum(i, k):
                    dve.wait_ge(rows_loaded[k], (i + 1) * 16)
                    dve.reduce_sum(part[:, 0, bass.ds(i * SLOTS + k, 1)], rows[:, k, 0:SPLIT], AX.X).then_inc(sum_v, 1)

                with dve.Fori(0, NTF) as i:
                    for k in range(SLOTS):
                        half_sum(i, k)
                for t in range(NTF * SLOTS, NT):
                    half_sum(NTF, t % SLOTS)
                dve.wait_ge(sum_v, NT)
                dve.wait_ge(sum_a, NT)
                link(dve.tensor_tensor(deg[:, :], part[:, 0, :], part[:, 1, :], ALU.add))
                dve.tensor_scalar(deg[:, :], deg[:, :], 1e-9, None, ALU.add).then_inc(deg_ready, 1)
                dve.wait_ge(dsq_ready, 1)
                link(dve.reciprocal(dinv[:, :], dsq[:, :]))
                dve.wait_ge(ln.xn_ready, NT)
                for t in range(NT):
                    dve.tensor_scalar(xn[:, t, :], xn[:, t, :], dinv[:, t:t + 1], None, ALU.mult)

            @block.scalar
            def _(act):
                ln.scalar(act)

                def half_sum(i, k):
                    act.wait_ge(rows_loaded[k], (i + 1) * 16)
                    act.wait_ge(ident_ready, 2)
                    act.activation(junk[:, :], rows[:, k, SPLIT:NP], ACT.Copy,
                                   accum_out=part[:, 1, bass.ds(i * SLOTS + k, 1)]).then_inc(sum_a, 1)
                    act.wait_ge(sum_a, i * SLOTS + k + 1)

                with act.Fori(0, NTF) as i:
                    for k in range(SLOTS):
                        half_sum(i, k)
                for t in range(NTF * SLOTS, NT):
                    half_sum(NTF, t % SLOTS)
                act.wait_ge(deg_ready, 1)
                act.activation(dsq[:, :], deg[:, :], ACT.Sqrt).then_inc(dsq_ready, 1)


def stage_gcn(nc, X, xn, dinv, adjT, wT, bias):
    PAIRS = NT // 2
    with ExitStack() as ctx:
        m = Mem(nc, ctx)
        ring = m.sb("gcn_ring", [P, PAIRS, 2, BLK])
        w_sb = m.sb("gcn_w", [P, DC, DM])
        b_sb = m.sb("gcn_b", [P, DM])
        hT = m.sb("gcn_hT", [P, 2, DC, BLK])
        y = m.sb("gcn_y", [P, SUB, DM])
        acc = m.ps("gcn_acc", [P, 2, DC, BLK])
        po = m.ps("gcn_po", [P, 2, 2, DM])
        w_loaded = m.sem("gcn_w_loaded")
        loaded = [m.sem(f"gcn_loaded{k}") for k in range(PAIRS)]
        pair_used = m.sem("gcn_pair_used")
        acc_full = m.sem("gcn_acc_full")
        hT_ready = m.sem("gcn_hT_ready")
        po_full = m.sem("gcn_po_full")
        po_read = m.sem("gcn_po_read")
        y_ready = m.sem("gcn_y_ready")
        src = adjT.rearrange("(k j p) i -> p k j i", p=P, j=2)
        NPAIR = NB // 2

        with nc.Block() as block:
            @block.sync
            def _(sp):
                sp.dma_start(w_sb[:, :, :], wT.rearrange("(c p) o -> p c o", p=P)).then_inc(w_loaded, 16)
                sp.dma_start(b_sb[:, :], row_on_all(bias)).then_inc(w_loaded, 16)
                for k in range(PAIRS):
                    sp.dma_start(ring[:, k, :, :], src[:, k, :, 0:BLK]).then_inc(loaded[k], 16)
                with sp.Fori(1, NB) as b:
                    for k in range(PAIRS):
                        sp.wait_ge(pair_used, (b - 1) * PAIRS + k + 1)
                        sp.dma_start(ring[:, k, :, :], src[:, k, :, bass.ds(b * BLK, BLK)]).then_inc(loaded[k], 16)
                for k in range(PAIRS):
                    sp.wait_ge(pair_used, (NB - 1) * PAIRS + k + 1)
                    sp.dma_start(ring[:, k, :, 0:TAIL], src[:, k, :, NB * BLK:NP]).then_inc(loaded[k], 16)

            @block.tensor
            def _(pe):
                pe.wait_ge(w_loaded, 32)

                def gather(b, q, w, first=False):
                    if not first:
                        pe.wait_ge(hT_ready, (b - 1) * DC)
                    for k in range(PAIRS):
                        pe.wait_ge(loaded[k], (b + 1) * 16)
                        for j in range(2):
                            for c in range(DC):
                                ins = pe.matmul(acc[:, q, c, 0:w], xn[:, 2 * k + j, c * P:(c + 1) * P],
                                                ring[:, k, j, 0:w], start=(k + j == 0),
                                                stop=(k == PAIRS - 1 and j == 1))
                        ins.then_inc(pair_used, 1)
                        if k == PAIRS - 1:
                            pass
                    pe.wait_ge(pair_used, (b + 1) * PAIRS)
                    pe.sem_inc(acc_full, 1)

                def project(b, q, w, first=False):
                    pe.wait_ge(hT_ready, (b + 1) * DC)
                    for s in range(w // P):
                        if not (first and s < 2):
                            pe.wait_ge(po_read, b * SUB + s - 1)
                        for c in range(DC):
                            ins = pe.matmul(po[:, s % 2, 0, :], hT[:, q, c, s * P:(s + 1) * P], w_sb[:, c, :],
                                            start=(c == 0), stop=(c == DC - 1))
                        ins.then_inc(po_full, 1)

                gather(0, 0, BLK, True)
                gather(1, 1, BLK, True)
                project(0, 0, BLK, True)
                with pe.Fori(1, NPAIR) as i:
                    gather(2 * i, 0, BLK)
                    project(2 * i - 1, 1, BLK)
                    gather(2 * i + 1, 1, BLK)
                    project(2 * i, 0, BLK)
                gather(NB, 0, TAIL)
                project(NB - 1, 1, BLK)
                project(NB, 0, TAIL)

            @block.scalar
            def _(act):
                def evac(b, q, w, first=False):
                    act.wait_ge(acc_full, b + 1)
                    if not first:
                        act.wait_ge(po_full, (b - 1) * SUB)
                    for c in range(DC):
                        act.activation(hT[:, q, c, 0:w], acc[:, q, c, 0:w], ACT.Copy).then_inc(hT_ready, 1)

                evac(0, 0, BLK, True)
                evac(1, 1, BLK, True)
                with act.Fori(1, NPAIR) as i:
                    evac(2 * i, 0, BLK)
                    evac(2 * i + 1, 1, BLK)
                evac(NB, 0, TAIL)

            @block.vector
            def _(dve):
                dve.wait_ge(w_loaded, 32)

                def finish(b, q, w, first=False):
                    for s in range(w // P):
                        t = b * SUB + s
                        dve.wait_ge(po_full, t + 1)
                        dve.scalar_tensor_tensor(y[:, s, :], po[:, s % 2, 0, :], dinv[:, bass.ds(t, 1)], b_sb[:, :],
                                                 ALU.mult, ALU.add).then_inc(po_read, 1)
                        dve.wait_ge(po_read, t + 1)
                        xt = X[:, bass.ds(t, 1), :].rearrange("p o d -> p (o d)")
                        dve.scalar_tensor_tensor(xt, y[:, s, :], 0.0, xt, ALU.max, ALU.add).then_inc(y_ready, 1)
                        dve.wait_ge(y_ready, t + 1)

                with dve.Fori(0, NB) as b:
                    finish(b, 0, BLK)
                finish(NB, 0, TAIL)


def stage_slices(nc, X, swT, tok, ident, w_x, w_sliceT, b_x, b_slice, temp):
    with ExitStack() as ctx:
        m = Mem(nc, ctx)
        xn = m.sb("sl_xn", [P, NT, DM + 1])
        xt = m.sb("sl_xt", [P, DC, NP])
        wx_sb = m.sb("sl_wx", [PH, H, DM])
        ws_sb = m.sb("sl_ws", [PH, G])
        bx_sb = m.sb("sl_bx", [PH, H])
        bx_all = m.sb("sl_bx_all", [PH, H, P])
        bs_sb = m.sb("sl_bs", [P, G])
        temp_sb = m.sb("sl_temp", [P, H])
        rtemp = m.sb("sl_rtemp", [P, H])
        wc = m.sb("sl_wc", [P, DC, HG])
        bias = m.sb("sl_bias", [P, HG])
        lg = m.sb("sl_lg", [P, 2, HG])
        ex = m.sb("sl_ex", [P, 2, HG])
        sw = m.sb("sl_sw", [P, 2, HG])
        mx = m.sb("sl_mx", [P, 2, H])
        sm = m.sb("sl_sum", [P, 2, H])
        rs = m.sb("sl_rsum", [P, 2, H])
        psL = m.ps("sl_psL", [P, 2, HG])
        psT = m.ps("sl_psT", [P, 2, HG])
        acc = m.ps("sl_acc", [P, KC, BLK])
        w_loaded = m.sem("sl_w_loaded")
        bx_ready = m.sem("sl_bx_ready")
        folded = m.sem("sl_folded")
        wc_ready = m.sem("sl_wc_ready")
        ones_ready = m.sem("sl_ones_ready")
        chain = m.sem("sl_chain")
        logits_full = m.sem("sl_logits_full")
        logits_read = m.sem("sl_logits_read")
        shifted = m.sem("sl_shifted")
        exped = m.sem("sl_exped")
        sw_ready = m.sem("sl_sw_ready")
        sw_turned = m.sem("sl_sw_turned")
        swT_ready = m.sem("sl_swT_ready")
        sw_used = m.sem("sl_sw_used")
        tok_ready = m.sem("sl_tok_ready")
        ln = LayerNorm(m, "ln1", X, xn, xt, ident, psT)
        N_LN = 2 * (NB + 1)

        def by_head(ap):
            return ap.rearrange("p (h g) -> p h g", g=G)

        def spread(ap):
            return ap.unsqueeze(2).broadcast_to([P, H, G])

        with nc.Block() as block:
            @block.sync
            def _(sp):
                sp.dma_start(wx_sb[:, :, :], w_x.rearrange("(h p) f -> p h f", p=PH)).then_inc(w_loaded, 16)
                sp.dma_start(ws_sb[:, :], w_sliceT).then_inc(w_loaded, 16)
                sp.dma_start(bx_sb[:, :], b_x).then_inc(w_loaded, 16)
                sp.dma_start(bs_sb[:, :], row_on_all(b_slice)).then_inc(w_loaded, 16)
                sp.dma_start(temp_sb[:, :], row_on_all(temp)).then_inc(w_loaded, 16)

            @block.gpsimd
            def _(pool):
                pool.memset(xn[:, :, DM:DM + 1], 1.0).then_inc(ones_ready, 1)

            @block.tensor
            def _(pe):
                pe.wait_ge(w_loaded, 80)
                for c in range(DC):
                    for h in range(H):
                        pe.matmul(acc[:, c, h * G:(h + 1) * G], wx_sb[:, h, c * P:(c + 1) * P], ws_sb[:, :],
                                  start=True, stop=True)
                pe.wait_ge(bx_ready, 1)
                for h in range(H):
                    ins = pe.matmul(acc[:, 2, h * G:(h + 1) * G], bx_all[:, h, :], ws_sb[:, :], start=True, stop=True)
                ins.then_inc(folded, 1)
                ln.tensor(pe)
                pe.wait_ge(wc_ready, 2)
                pe.wait_ge(ln.xt_ready, N_LN)
                pe.wait_ge(ones_ready, 1)

                def logits(t):
                    if t >= 2:
                        pe.wait_ge(logits_read, t - 1)
                    for c in range(DC):
                        ins = pe.matmul(psL[:, t % 2, :], xt[:, c, t * P:(t + 1) * P], wc[:, c, :],
                                        start=(c == 0), stop=(c == DC - 1))
                    ins.then_inc(logits_full, 1)

                def gather(t):
                    rows = P if t < NT - 1 else LAST
                    pe.wait_ge(sw_ready, t + 1)
                    if t >= 2:
                        pe.wait_ge(swT_ready, t - 1)
                    for k in range(KC):
                        ins = pe.transpose(psT[:, t % 2, k * P:(k + 1) * P], sw[:, t % 2, k * P:(k + 1) * P], ident[:, :])
                    ins.then_inc(sw_turned, 1)
                    for k in range(KC):
                        ins = pe.matmul(acc[:, k, 0:DM + 1], sw[0:rows, t % 2, k * P:(k + 1) * P], xn[0:rows, t, :],
                                        start=(t == 0), stop=(t == NT - 1))
                    ins.then_inc(sw_used, 1)

                logits(0)
                logits(1)
                for t in range(NT):
                    gather(t)
                    if t + 2 < NT:
                        logits(t + 2)

            @block.vector
            def _(dve):
                link = Linker(dve, chain)
                dve.wait_ge(w_loaded, 80)
                dve.tensor_copy(bx_all[:, :, :], bx_sb[:, :].unsqueeze(2).broadcast_to([PH, H, P])).then_inc(bx_ready, 1)
                link(dve.tensor_scalar(temp_sb[:, :], temp_sb[:, :], 1e-6, None, ALU.max))
                link(dve.reciprocal(rtemp[:, :], temp_sb[:, :]))
                dve.wait_ge(folded, 1)
                for c in range(DC):
                    ins = dve.tensor_tensor(by_head(wc[:, c, :]), by_head(acc[:, c, :]), spread(rtemp[:, :]), ALU.mult)
                ins.then_inc(wc_ready, 1)
                link(dve.tensor_tensor(by_head(bias[:, :]), by_head(acc[:, 2, :]),
                                       bs_sb[:, :].unsqueeze(1).broadcast_to([P, H, G]), ALU.add))
                link(dve.tensor_tensor(by_head(bias[:, :]), by_head(bias[:, :]), spread(rtemp[:, :]), ALU.mult))
                dve.sem_inc(wc_ready, 1)
                ln.vector(dve, link)

                def shift(t):
                    q = t % 2
                    dve.wait_ge(logits_full, t + 1)
                    dve.tensor_tensor(lg[:, q, :], psL[:, q, :], bias[:, :], ALU.add).then_inc(logits_read, 1)
                    dve.wait_ge(logits_read, t + 1)
                    link(dve.tensor_reduce(mx[:, q, :], by_head(lg[:, q, :]), AX.X, ALU.max))
                    if t >= 2:
                        dve.wait_ge(exped, t - 1)
                    dve.tensor_tensor(by_head(lg[:, q, :]), by_head(lg[:, q, :]), spread(mx[:, q, :]),
                                      ALU.subtract).then_inc(shifted, 1)

                def normalise(t):
                    q = t % 2
                    dve.wait_ge(exped, t + 1)
                    link(dve.tensor_reduce(sm[:, q, :], by_head(ex[:, q, :]), AX.X, ALU.add))
                    link(dve.reciprocal(rs[:, q, :], sm[:, q, :]))
                    if t >= 2:
                        dve.wait_ge(sw_used, t - 1)
                    dve.tensor_tensor(by_head(sw[:, q, :]), by_head(ex[:, q, :]), spread(rs[:, q, :]),
                                      ALU.mult).then_inc(sw_ready, 1)

                shift(0)
                for t in range(NT):
                    if t + 1 < NT:
                        shift(t + 1)
                    normalise(t)
                dve.wait_ge(sw_used, NT)
                for k in range(KC):
                    dve.tensor_copy(tok[:, k, :], acc[:, k, 0:DM + 1]).then_inc(tok_ready, 1)

            @block.scalar
            def _(act):
                ln.scalar(act)
                for t in range(NT + 1):
                    if t < NT:
                        act.wait_ge(shifted, t + 1)
                        if t >= 2:
                            act.wait_ge(sw_ready, t - 1)
                        act.activation(ex[:, t % 2, :], lg[:, t % 2, :], ACT.Exp).then_inc(exped, 1)
                    if t >= 1:
                        u = t - 1
                        act.wait_ge(sw_turned, u + 1)
                        act.activation(swT[:, :, u * P:(u + 1) * P],
                                       psT[:, u % 2, :].rearrange("p (k i) -> p k i", k=KC), ACT.Copy).then_inc(swT_ready, 1)


DI = H * PH
XC = DI // P
TAPS = 3
ST = 64
DTW = 2 * H


def stage_hydra(nc, X, swT, tok, ident, io):
    L = G
    GR = XC + 2
    with ExitStack() as ctx:
        m = Mem(nc, ctx)
        wfx = m.sb("hy_wfx", [P, DC, DI])
        bfx = m.sb("hy_bfx", [1, DI])
        w_in = m.sb("hy_win", [P, XC, 2 * DI + 2 * ST + DTW])
        cw = m.sb("hy_cw", [P, GR, TAPS])
        cb = m.sb("hy_cb", [P, GR])
        dtb = m.sb("hy_dtb", [L, H])
        alog = m.sb("hy_alog", [L, H])
        dD = m.sb("hy_D", [L, H])
        fcd = m.sb("hy_fcd", [P, XC, H])
        nw = m.sb("hy_nw", [P, XC])
        w_hy = m.sb("hy_wout", [P, XC, DI])
        w_o = m.sb("hy_wo", [P, XC, DM])
        ob = m.sb("hy_ob", [P, DM])
        den = m.sb("hy_den", [P, KC])
        rden = m.sb("hy_rden", [P, KC])
        tn = m.sb("hy_tn", [P, KC, DM + 1])
        tnT = m.sb("hy_tnT", [P, DC, HG])
        rT = m.sb("hy_rT", [1, HG])
        uT = m.sb("hy_uT", [P, XC, L])
        z = m.sb("hy_z", [L, DI])
        zs = m.sb("hy_zs", [L, DI])
        raw = m.sb("hy_raw", [P, GR, L + TAPS - 1])
        cv = m.sb("hy_cv", [P, GR, L])
        cs = m.sb("hy_cs", [P, GR, L])
        xbc = m.sb("hy_xbc", [P, GR, L])
        xr = m.sb("hy_xr", [L, DI])
        dt = m.sb("hy_dt", [L, 2, H])
        dta = m.sb("hy_dta", [L, 2, H])
        dtp = m.sb("hy_dtp", [L, 2, H])
        a = m.sb("hy_a", [L, 2, H])
        ea = m.sb("hy_ea", [L, H])
        m_after = m.sb("hy_m_after", [L, 2, L])
        m_upto = m.sb("hy_m_upto", [L, 2, L])
        arow = m.sb("hy_arow", [L, 2, H, L])
        decay = m.sb("hy_decay", [L, 2, H, L])
        cbm = m.sb("hy_cbm", [L, 2, L])
        wts = m.sb("hy_wts", [L, 2, H, L])
        y = m.sb("hy_y", [L, DI])
        sk = m.sb("hy_sk", [L, H])
        sq = m.sb("hy_sq", [L, DI])
        ms = m.sb("hy_ms", [L, 4])
        ygT = m.sb("hy_ygT", [P, XC, L])
        otT = m.sb("hy_otT", [P, XC, L])
        mix = m.sb("hy_mix", [P, KC, DM])
        psA = m.ps("hy_psA", [P, BLK])
        psB = m.ps("hy_psB", [P, BLK])
        psC = m.ps("hy_psC", [P, BLK])
        psD = m.ps("hy_psD", [P, 2, BLK])
        psE = m.ps("hy_psE", [P, BLK])
        po = m.ps("hy_po", [P, 2, BLK])
        w_loaded = m.sem("hy_w_loaded")
        p_step = m.sem("hy_p_step")
        v_step = m.sem("hy_v_step")
        a_step = m.sem("hy_a_step")
        masks = m.sem("hy_masks")
        dt_ready = m.sem("hy_dt_ready")
        ms_ready = m.sem("hy_ms_ready")
        chain = m.sem("hy_chain")
        ob_added = m.sem("hy_ob_added")
        po_full = m.sem("hy_po_full")
        x_added = m.sem("hy_x_added")
        xcat = 2 * DI + 2 * ST

        def heads(ap, w):
            return ap.rearrange("p (h w) -> p h w", w=w)

        with nc.Block() as block:
            @block.sync
            def _(sp):
                chunked = "(c p) o -> p c o"
                for dst, src in ((wfx[:, :, :], io["w_fxT"].rearrange(chunked, p=P)),
                                 (bfx[:, :], io["b_fx"].unsqueeze(0)),
                                 (w_in[:, :, :], io["in_wT"].rearrange(chunked, p=P)),
                                 (cw[:, 0:XC, :], io["conv_w"][0:DI, :].rearrange(chunked, p=P)),
                                 (cw[0:ST, XC:GR, :], io["conv_w"][DI:DI + 2 * ST, :].rearrange(chunked, p=ST)),
                                 (cb[:, :], io["conv_b"]),
                                 (dtb[:, :], row_on_all(io["dt_bias"], L)),
                                 (alog[:, :], row_on_all(io["A_log"], L)),
                                 (dD[:, :], row_on_all(io["D"], L)),
                                 (fcd[:, :, :], io["fcD_wT"].rearrange(chunked, p=P)),
                                 (nw[:, :], io["norm_w"]),
                                 (w_hy[:, :, :], io["hy_outT"].rearrange(chunked, p=P)),
                                 (w_o[:, :, :], io["out_wT"].rearrange(chunked, p=P)),
                                 (ob[:, :], row_on_all(io["out_b"]))):
                    sp.dma_start(dst, src).then_inc(w_loaded, 16)

            W_ALL = 14 * 16

            @block.gpsimd
            def _(pool):
                n = 0

                def step(ins):
                    nonlocal n
                    n += 1
                    ins.then_inc(masks, 1)
                    pool.wait_ge(masks, n)

                step(pool.memset(m_after[:, :, :], 1.0))
                step(pool.memset(m_upto[:, :, :], 1.0))
                step(pool.memset(raw[:, :, 0:TAPS - 1], 0.0))
                step(pool.affine_select(out=m_after[:, 0, :], in_=m_after[:, 0, :], compare_op=ALU.is_gt, fill=0.0,
                                        base=0, pattern=[[-1, L]], channel_multiplier=1))
                step(pool.affine_select(out=m_after[:, 1, :], in_=m_after[:, 1, :], compare_op=ALU.is_gt, fill=0.0,
                                        base=0, pattern=[[1, L]], channel_multiplier=-1))
                step(pool.affine_select(out=m_upto[:, 0, :], in_=m_upto[:, 0, :], compare_op=ALU.is_gt, fill=0.0,
                                        base=0, pattern=[[1, L]], channel_multiplier=-1))
                step(pool.affine_select(out=m_upto[:, 1, :], in_=m_upto[:, 1, :], compare_op=ALU.is_gt, fill=0.0,
                                        base=0, pattern=[[-1, L]], channel_multiplier=1))
                pool.wait_ge(w_loaded, W_ALL)
                for t in range(NT):
                    pool.tensor_tensor(X[:, t, :], X[:, t, :], ob[:, :], ALU.add).then_inc(ob_added, 1)

            @block.tensor
            def _(pe):
                n = 0

                def done(ins):
                    nonlocal n
                    n += 1
                    ins.then_inc(p_step, 1)

                pe.wait_ge(w_loaded, W_ALL)
                pe.wait_ge(v_step, 1)
                for c in range(DC):
                    for k in range(KC):
                        ins = pe.transpose((psA, psB)[c][:, k * P:(k + 1) * P], tn[:, k, c * P:(c + 1) * P], ident[:, :])
                    done(ins)
                for k in range(KC):
                    ins = pe.transpose(psC[0:1, k * P:(k + 1) * P], tn[:, k, DM:DM + 1], ident[:, :])
                done(ins)
                pe.wait_ge(v_step, 4)
                for h in range(H):
                    o = psE[(h % 2) * PH:(h % 2 + 1) * PH, (h // 2) * L:(h // 2 + 1) * L]
                    for c in range(DC):
                        pe.matmul(o, wfx[:, c, h * PH:(h + 1) * PH], tnT[:, c, h * G:(h + 1) * G],
                                  start=(c == 0), stop=False)
                    ins = pe.matmul(o, bfx[:, h * PH:(h + 1) * PH], rT[:, h * G:(h + 1) * G], start=False, stop=True)
                done(ins)
                pe.wait_ge(v_step, 5)
                for g in range(GR):
                    w = P if g < XC else ST
                    c0 = DI + (g * P if g < XC else DI + (g - XC) * ST)
                    for k in range(XC):
                        ins = pe.matmul(psA[0:w, g * L:(g + 1) * L], w_in[:, k, c0:c0 + w], uT[:, k, :],
                                        start=(k == 0), stop=(k == XC - 1))
                done(ins)
                for k in range(XC):
                    ins = pe.matmul(po[0:L, 0, 0:DTW], uT[:, k, :], w_in[:, k, xcat:xcat + DTW],
                                    start=(k == 0), stop=(k == XC - 1))
                done(ins)
                for k in range(XC):
                    ins = pe.matmul(psB[0:L, :], uT[:, k, :], w_in[:, k, 0:DI], start=(k == 0), stop=(k == XC - 1))
                done(ins)
                pe.wait_ge(v_step, 7)
                done(pe.matmul(psC[0:L, 64:64 + L], xbc[0:ST, XC, :], xbc[0:ST, XC + 1, :], start=True, stop=True))
                for k in range(XC):
                    ins = pe.transpose(psE[0:L, k * P:(k + 1) * P], xbc[:, k, :], ident[:, :])
                done(ins)
                for k in range(XC):
                    ins = pe.matmul(psC[0:L, 192:192 + H], xbc[:, k, :], fcd[:, k, :], start=(k == 0), stop=(k == XC - 1))
                done(ins)
                pe.wait_ge(v_step, 8)
                for d in range(2):
                    ins = pe.matmul(psD[0:L, d, :], m_after[:, d, :], arow[:, d, :, :].rearrange("r h t -> r (h t)"),
                                    start=True, stop=True)
                done(ins)
                pe.wait_ge(v_step, 9)
                for h in range(H):
                    ins = pe.matmul(psA[0:L, h * PH:(h + 1) * PH], wts[:, 0, h, :], xr[:, h * PH:(h + 1) * PH],
                                    start=True, stop=True)
                done(ins)
                pe.wait_ge(v_step, 10)
                for k in range(XC):
                    ins = pe.transpose(psC[:, k * L:(k + 1) * L], y[:, k * P:(k + 1) * P], ident[0:L, 0:L])
                done(ins)
                pe.wait_ge(v_step, 11)
                for e in range(XC):
                    for k in range(XC):
                        ins = pe.matmul(psE[:, e * L:(e + 1) * L], w_hy[:, k, e * P:(e + 1) * P], ygT[:, k, :],
                                        start=(k == 0), stop=(k == XC - 1))
                done(ins)
                pe.wait_ge(v_step, 12)
                for h in range(H):
                    r0 = (h % 2) * PH
                    ins = pe.matmul((psA, psB)[h // 4][r0:r0 + PH, ((h // 2) % 2) * DM:((h // 2) % 2 + 1) * DM],
                                    otT[r0:r0 + PH, h // 2, :], w_o[r0:r0 + PH, h // 2, :], start=True, stop=True)
                done(ins)
                pe.wait_ge(v_step, 13)
                for t in range(NT):
                    if t >= 2:
                        pe.wait_ge(x_added, t - 1)
                    for k in range(KC):
                        ins = pe.matmul(po[:, t % 2, 0:DM], swT[:, k, t * P:(t + 1) * P], mix[:, k, :],
                                        start=(k == 0), stop=(k == KC - 1))
                    ins.then_inc(po_full, 1)

            @block.vector
            def _(dve):
                link = Linker(dve, chain)
                dve.wait_ge(w_loaded, W_ALL)
                link(dve.tensor_scalar(den[:, :], tok[:, :, DM], 1e-5, None, ALU.add))
                link(dve.reciprocal(rden[:, :], den[:, :]))
                link(dve.tensor_tensor(tn[:, :, :], tok[:, :, :], rden[:, :].unsqueeze(2).broadcast_to([P, KC, DM + 1]),
                                       ALU.mult))
                dve.sem_inc(v_step, 1)
                dve.wait_ge(p_step, 1)
                dve.tensor_copy(tnT[:, 0, :], psA[:, :]).then_inc(v_step, 1)
                dve.wait_ge(p_step, 2)
                dve.tensor_copy(tnT[:, 1, :], psB[:, :]).then_inc(v_step, 1)
                dve.wait_ge(p_step, 3)
                dve.tensor_copy(rT[:, :], psC[0:1, :]).then_inc(v_step, 1)
                dve.wait_ge(p_step, 4)
                dve.tensor_copy(uT[:, :, :], psE[:, 0:XC * L].rearrange("p (k l) -> p k l", l=L)).then_inc(v_step, 1)
                dve.wait_ge(p_step, 5)
                dve.wait_ge(masks, 3)
                link(dve.tensor_copy(raw[:, 0:XC, TAPS - 1:], psA[:, 0:XC * L].rearrange("p (k l) -> p k l", l=L)))
                link(dve.tensor_copy(raw[0:ST, XC:GR, TAPS - 1:],
                                     psA[0:ST, XC * L:GR * L].rearrange("p (k l) -> p k l", l=L)))
                for g in range(GR):
                    w = P if g < XC else ST
                    link(dve.tensor_scalar(cv[0:w, g, :], raw[0:w, g, 0:L], cw[0:w, g, 0:1], cb[0:w, g:g + 1],
                                           ALU.mult, ALU.add))
                    for k in range(1, TAPS):
                        link(dve.scalar_tensor_tensor(cv[0:w, g, :], raw[0:w, g, k:k + L], cw[0:w, g, k:k + 1],
                                                      cv[0:w, g, :], ALU.mult, ALU.add))
                dve.sem_inc(v_step, 1)
                dve.wait_ge(a_step, 1)
                link(dve.tensor_tensor(xbc[:, 0:XC, :], cv[:, 0:XC, :], cs[:, 0:XC, :], ALU.mult))
                link(dve.tensor_tensor(xbc[0:ST, XC:GR, :], cv[0:ST, XC:GR, :], cs[0:ST, XC:GR, :], ALU.mult))
                dve.sem_inc(v_step, 1)
                dve.wait_ge(p_step, 6)
                link(dve.tensor_tensor(dt[:, :, :], po[0:L, 0, 0:DTW].rearrange("s (d h) -> s d h", h=H),
                                       dtb[:, :].unsqueeze(1).broadcast_to([L, 2, H]), ALU.add))
                link(dve.tensor_scalar(dtp[:, :, :], dt[:, :, :], -1.0, None, ALU.mult))
                dve.tensor_tensor(dta[:, :, :], dt[:, :, :], dtp[:, :, :], ALU.min).then_inc(dt_ready, 1)
                dve.wait_ge(a_step, 3)
                dve.tensor_scalar(dtp[:, :, :], dta[:, :, :], 1.0, None, ALU.add).then_inc(dt_ready, 1)
                dve.wait_ge(a_step, 4)
                link(dve.scalar_tensor_tensor(dt[:, :, :], dt[:, :, :], 0.0, dtp[:, :, :], ALU.max, ALU.add))
                link(dve.tensor_scalar(ea[:, :], ea[:, :], 1e30, -1.0, ALU.min, ALU.mult))
                link(dve.tensor_tensor(a[:, :, :], dt[:, :, :], ea[:, :].unsqueeze(1).broadcast_to([L, 2, H]), ALU.mult))
                dve.wait_ge(masks, 7)
                for d in range(2):
                    link(dve.tensor_tensor(arow[:, d, :, :], m_upto[:, d, :].unsqueeze(1).broadcast_to([L, H, L]),
                                           a[:, d, :].unsqueeze(2).broadcast_to([L, H, L]), ALU.mult))
                dve.sem_inc(v_step, 1)
                dve.wait_ge(p_step, 10)
                link(dve.memset(cbm[:, :, :], 0.0))
                link(dve.tensor_tensor(cbm[:, 0, 1:L], psC[0:L, 64:64 + L - 1], m_upto[:, 0, 1:L], ALU.mult))
                link(dve.tensor_tensor(cbm[:, 1, 0:L - 1], psC[0:L, 65:64 + L], m_upto[:, 1, 0:L - 1], ALU.mult))
                for d in range(2):
                    link(dve.tensor_tensor(wts[:, d, :, :], cbm[:, d, :].unsqueeze(1).broadcast_to([L, H, L]),
                                           dt[:, d, :].unsqueeze(2).broadcast_to([L, H, L]), ALU.mult))
                dve.wait_ge(p_step, 9)
                link(dve.tensor_copy(xr[:, :], psE[0:L, :]))
                dve.wait_ge(a_step, 5)
                link(dve.tensor_tensor(wts[:, :, :, :].rearrange("s d h t -> s (d h t)"),
                                       wts[:, :, :, :].rearrange("s d h t -> s (d h t)"),
                                       decay[:, :, :, :].rearrange("s d h t -> s (d h t)"), ALU.mult))
                link(dve.tensor_tensor(wts[:, 0, :, :], wts[:, 0, :, :], wts[:, 1, :, :], ALU.add))
                dve.sem_inc(v_step, 1)
                dve.wait_ge(p_step, 12)
                link(dve.tensor_tensor(sk[:, :], psC[0:L, 192:192 + H], dD[:, :], ALU.add))
                link(dve.tensor_tensor(heads(sq[:, :], PH), heads(xr[:, :], PH), sk[:, :].unsqueeze(2).broadcast_to([L, H, PH]),
                                       ALU.mult))
                link(dve.tensor_tensor(y[:, :], psA[0:L, :], sq[:, :], ALU.add))
                link(dve.tensor_tensor(y[:, :], y[:, :], z[:, :], ALU.mult))
                link(dve.tensor_tensor(y[:, :], y[:, :], zs[:, :], ALU.mult))
                link(dve.tensor_tensor(sq[:, :], y[:, :], y[:, :], ALU.mult))
                link(dve.reduce_sum(ms[:, 0:1], sq[:, :], AX.X))
                link(dve.tensor_scalar(ms[:, 1:2], ms[:, 0:1], 1.0 / DI, 1e-5, ALU.mult, ALU.add))
                dve.sem_inc(ms_ready, 1)
                dve.wait_ge(a_step, 6)
                link(dve.reciprocal(ms[:, 3:4], ms[:, 2:3]))
                link(dve.tensor_scalar(y[:, :], y[:, :], ms[:, 3:4], None, ALU.mult))
                dve.sem_inc(v_step, 1)
                dve.wait_ge(p_step, 13)
                for k in range(XC):
                    link(dve.tensor_scalar(ygT[:, k, :], psC[:, k * L:(k + 1) * L], nw[:, k:k + 1], None, ALU.mult))
                dve.sem_inc(v_step, 1)
                dve.wait_ge(p_step, 14)
                dve.tensor_copy(otT[:, :, :], psE[:, 0:XC * L].rearrange("p (k l) -> p k l", l=L)).then_inc(v_step, 1)
                dve.wait_ge(p_step, 15)
                for i, ps in enumerate((psA, psB)):
                    link(dve.tensor_copy(mix[:, 2 * i:2 * i + 2, :], ps[:, :].rearrange("p (k o) -> p k o", o=DM)))
                dve.sem_inc(v_step, 1)
                dve.wait_ge(ob_added, NT)
                for t in range(NT):
                    dve.wait_ge(po_full, t + 1)
                    dve.tensor_tensor(X[:, t, :], X[:, t, :], po[:, t % 2, 0:DM], ALU.add).then_inc(x_added, 1)

            @block.scalar
            def _(act):
                act.wait_ge(v_step, 6)
                act.activation(cs[:, 0:XC, :], cv[:, 0:XC, :], ACT.Sigmoid)
                act.activation(cs[0:ST, XC:GR, :], cv[0:ST, XC:GR, :], ACT.Sigmoid).then_inc(a_step, 1)
                act.wait_ge(p_step, 7)
                act.activation(z[:, :], psB[0:L, :], ACT.Copy)
                act.activation(zs[:, :], psB[0:L, :], ACT.Sigmoid).then_inc(a_step, 1)
                act.wait_ge(dt_ready, 1)
                act.activation(dta[:, :, :], dta[:, :, :], ACT.Exp)
                act.activation(ea[:, :], alog[:, :], ACT.Exp).then_inc(a_step, 1)
                act.wait_ge(dt_ready, 2)
                act.activation(dtp[:, :, :], dtp[:, :, :], ACT.Ln).then_inc(a_step, 1)
                act.wait_ge(p_step, 11)
                act.activation(decay[:, :, :, :].rearrange("s d h t -> s (d h t)"),
                               psD[0:L, :, :].rearrange("s d n -> s (d n)"), ACT.Exp).then_inc(a_step, 1)
                act.wait_ge(ms_ready, 1)
                act.activation(ms[:, 2:3], ms[:, 1:2], ACT.Sqrt).then_inc(a_step, 1)


def by_group(v):
    top = v[:DI].reshape(XC, P)
    rest = np.pad(v[DI:].reshape(2, ST), ((0, 0), (0, P - ST)))
    return np.concatenate([top, rest]).T


SLOPE = 0.2


def stage_gat_prepare(nc, X, h1, f1_all, f2_all, f18, f28, f20, ident, all_ones, weight, weightT, conv12, bias):
    with ExitStack() as ctx:
        m = Mem(nc, ctx)
        xn = m.sb("gp_xn", [P, NT, DM])
        xt = m.sb("gp_xt", [P, DC, NP])
        w3 = m.sb("gp_w3", [P, DC, DM + 2])
        wT_sb = m.sb("gp_wT", [P, DC, DM])
        c12 = m.sb("gp_c12", [P, DC, 2])
        b_sb = m.sb("gp_b", [P, DM])
        wall = m.sb("gp_wall", [P, DC, 2, P])
        f12 = m.sb("gp_f12", [P, NT, 2])
        psT = m.ps("gp_psT", [P, 2, BLK])
        psW = m.ps("gp_psW", [P, BLK])
        psH = m.ps("gp_psH", [P, 2, BLK])
        psF = m.ps("gp_psF", [P, 2, BLK])
        w_loaded = m.sem("gp_w_loaded")
        folded = m.sem("gp_folded")
        w3_ready = m.sem("gp_w3_ready")
        wall_ready = m.sem("gp_wall_ready")
        h_full = m.sem("gp_h_full")
        h_read = m.sem("gp_h_read")
        f_full = m.sem("gp_f_full")
        f_read = m.sem("gp_f_read")
        chain = m.sem("gp_chain")
        ones = m.sem("gp_ones")
        biased = m.sem("gp_biased")
        ln = LayerNorm(m, "ln2", X, xn, xt, ident, psT)
        rows = [(z, c0, w) for z in range(2) for c0, w in blocks_of_tokens()]

        with nc.Block() as block:
            @block.sync
            def _(sp):
                sp.dma_start(w3[:, :, 0:DM], weight.rearrange("(c p) o -> p c o", p=P)).then_inc(w_loaded, 16)
                sp.dma_start(wT_sb[:, :, :], weightT.rearrange("(c p) o -> p c o", p=P)).then_inc(w_loaded, 16)
                sp.dma_start(c12[:, :, :], conv12.rearrange("(c p) o -> p c o", p=P)).then_inc(w_loaded, 16)
                sp.dma_start(b_sb[:, :], row_on_all(bias)).then_inc(w_loaded, 16)

            @block.gpsimd
            def _(pool):
                pool.memset(h1[:, :, DM:DM + 1], 1.0).then_inc(ones, 1)
                pool.memset(all_ones[:, :], 1.0).then_inc(ones, 1)
                pool.wait_ge(w_loaded, 64)
                pool.wait_ge(ln.xn_ready, NT)
                for t in range(NT):
                    pool.tensor_tensor(X[:, t, :], X[:, t, :], b_sb[:, :], ALU.add).then_inc(biased, 1)

            @block.tensor
            def _(pe):
                pe.wait_ge(w_loaded, 64)
                for c in range(DC):
                    for k in range(DC):
                        ins = pe.matmul(psW[:, 2 * c:2 * c + 2], wT_sb[:, k, c * P:(c + 1) * P], c12[:, k, :],
                                        start=(k == 0), stop=(k == DC - 1))
                ins.then_inc(folded, 1)
                ln.tensor(pe)
                pe.wait_ge(w3_ready, 1)
                pe.wait_ge(ln.xt_ready, 2 * (NB + 1))
                pe.wait_ge(wall_ready, 1)
                for n, (z, c0, w) in enumerate(rows):
                    if n >= 2:
                        pe.wait_ge(f_read, n - 1)
                    for c in range(DC):
                        ins = pe.matmul(psF[:, n % 2, 0:w], wall[:, c, z, :], xt[:, c, c0:c0 + w],
                                        start=(c == 0), stop=(c == DC - 1))
                    ins.then_inc(f_full, 1)
                for t in range(NT):
                    if t >= 2:
                        pe.wait_ge(h_read, t - 1)
                    for c in range(DC):
                        ins = pe.matmul(psH[:, t % 2, 0:DM + 2], xt[:, c, t * P:(t + 1) * P], w3[:, c, :],
                                        start=(c == 0), stop=(c == DC - 1))
                    ins.then_inc(h_full, 1)

            @block.vector
            def _(dve):
                link = Linker(dve, chain)
                dve.wait_ge(folded, 1)
                dve.wait_ge(w_loaded, 64)
                dve.tensor_copy(w3[:, :, DM:DM + 2], psW[:, 0:2 * DC].rearrange("p (c z) -> p c z", z=2)).then_inc(w3_ready, 1)
                dve.wait_ge(w3_ready, 1)
                dve.tensor_copy(wall[:, :, :, :].rearrange("p c z q -> p (c z) q"),
                                psW[:, 0:2 * DC].unsqueeze(2).broadcast_to([P, 2 * DC, P])).then_inc(wall_ready, 1)
                ln.vector(dve, link)
                for t in range(NT):
                    dve.wait_ge(h_full, t + 1)
                    dve.tensor_copy(h1[:, t, 0:DM], psH[:, t % 2, 0:DM])
                    dve.tensor_copy(f12[:, t, :], psH[:, t % 2, DM:DM + 2]).then_inc(h_read, 1)
                dve.wait_ge(h_read, NT)
                dve.tensor_scalar(f18[:, :], f12[:, :, 0], 1.0 - SLOPE, None, ALU.mult)
                dve.tensor_scalar(f28[:, :], f12[:, :, 1], 1.0 - SLOPE, None, ALU.mult)
                dve.tensor_scalar(f20[:, :], f12[:, :, 1], SLOPE, None, ALU.mult)

            @block.scalar
            def _(act):
                ln.scalar(act)
                for n, (z, c0, w) in enumerate(rows):
                    act.wait_ge(f_full, n + 1)
                    act.activation((f1_all, f2_all)[z][:, c0:c0 + w], psF[:, n % 2, 0:w], ACT.Copy).then_inc(f_read, 1)


def stage_gat(nc, X, h1, f1_all, f2_all, f18, f28, f20, ident, ones, adj, adjT):
    PAIRS = NT // 2
    MAX_AFTER = (0, 3, 5, 8)
    BC_AFTER = 9
    NM_AFTER = 10
    AHEAD_RELU, AHEAD_SUM, AHEAD_SHIFT = 4, 3, 2
    with ExitStack() as ctx:
        m = Mem(nc, ctx)
        ring = m.sb("ga_ring", [P, PAIRS, 2, BLK])
        rows = m.sb("ga_rows", [P, 2, NP])
        rl = m.sb("ga_rl", [P, 2, NP])
        rp = m.sb("ga_rp", [P, 2, 2, BLK])
        mcol = m.sb("ga_mcol", [P, SUB])
        pace_a = m.sb("ga_pace_a", [P, 2 * PAIRS + SUB])
        pace_v = m.sb("ga_pace_v", [P, SUB])
        diag = m.sb("ga_diag", [P, SUB, P])
        nm = m.sb("ga_nm", [P, 2, BLK])
        rs = m.sb("ga_rs", [P, SUB])
        acc = m.ps("ga_acc", [P, SUB, BLK])
        psM = m.ps("ga_psM", [P, BLK])
        pair_loaded = [m.sem(f"ga_pair_loaded{k}") for k in range(PAIRS)]
        rows_loaded = [m.sem(f"ga_rows_loaded{k}") for k in range(2)]
        row_relu = m.sem("ga_row_relu")
        row_sum = m.sem("ga_row_sum")
        row_max = m.sem("ga_row_max")
        diag_ready = m.sem("ga_diag_ready")
        m_spread = m.sem("ga_m_spread")
        nm_ready = m.sem("ga_nm_ready")
        relu_ready = m.sem("ga_relu_ready")
        sum_ready = m.sem("ga_sum_ready")
        shift_ready = m.sem("ga_shift_ready")
        exp_ready = m.sem("ga_exp_ready")
        pair_used = m.sem("ga_pair_used")
        acc_full = m.sem("ga_acc_full")
        rs_ready = m.sem("ga_rs_ready")
        acc_read = m.sem("ga_acc_read")
        srcT = adjT.rearrange("(k j p) i -> p k j i", p=P, j=2)

        def passes(eng, block_fn, start):
            start()
            turns = NB // 2 - 1
            with eng.Fori(0, turns) as i:
                block_fn(2 * i, 0, BLK, BLK)
                block_fn(2 * i + 1, 1, BLK, BLK)
            block_fn(2 * turns, 0, BLK, BLK)
            block_fn(2 * turns + 1, 1, BLK, TAIL)
            block_fn(NB, 0, TAIL, 0)

        def ahead(b, q, w, w_next, k, n):
            if k + n < PAIRS:
                return b, q, w, k + n
            return (b + 1, 1 - q, w_next, k + n - PAIRS) if w_next else None

        with nc.Block() as block:
            @block.sync
            def _(sp):
                def load_rows(b, s, first=False):
                    t = b * SUB + s
                    if not first:
                        sp.wait_ge(row_max, t - 1)
                    sp.dma_start(rows[:, s % 2, :], adj[bass.ds(t * P, P), :]).then_inc(rows_loaded[s % 2], 16)

                def load_pair(b, w, k, first=False):
                    if not first:
                        sp.wait_ge(pair_used, (b - 1) * PAIRS + k + 1)
                    sp.dma_start(ring[:, k, :, 0:w], srcT[:, k, :, bass.ds(b * BLK, w)]).then_inc(pair_loaded[k], 16)

                def one(b, q, w, w_next):
                    for k in range(PAIRS):
                        if k in MAX_AFTER and w_next and MAX_AFTER.index(k) < w_next // P:
                            load_rows(b + 1, MAX_AFTER.index(k))
                        if w_next:
                            load_pair(b + 1, w_next, k)

                def start():
                    for s in range(SUB):
                        load_rows(0, s, s < 2)
                        if s == 1:
                            for k in range(PAIRS):
                                load_pair(0, BLK, k, True)

                passes(sp, one, start)

            @block.scalar
            def _(act):
                def rows_relu(b, s, first=False):
                    t = b * SUB + s
                    if not first:
                        act.wait_ge(row_max, t - 1)
                    act.activation(pace_a[:, 2 * PAIRS + s:2 * PAIRS + s + 1], f20[:, 0:1], ACT.Copy)
                    act.activation(rl[:, s % 2, 0:N], f2_all[:, 0:N], ACT.Relu, bias=f18[:, bass.ds(t, 1)],
                                   scale=1.0 - SLOPE).then_inc(row_relu, 1)

                def pair_relu(b, q, w, k, first=False):
                    slot = (q * PAIRS + k) % 2
                    if not first:
                        act.wait_ge(sum_ready, b * PAIRS + k - 1)
                    act.activation(pace_a[:, q * PAIRS + k:q * PAIRS + k + 1], f20[:, 0:1], ACT.Copy)
                    for j in range(2):
                        ins = act.activation(rp[:, slot, j, 0:w], f1_all[:, bass.ds(b * BLK, w)], ACT.Relu,
                                             bias=f28[:, 2 * k + j:2 * k + j + 1], scale=1.0 - SLOPE)
                    ins.then_inc(relu_ready, 1)

                def spread_copy(b, q, w):
                    act.wait_ge(m_spread, b + 1)
                    act.activation(nm[:, q, 0:w], psM[:, 0:w], ACT.Copy).then_inc(nm_ready, 1)

                def one(b, q, w, w_next):
                    for k in range(PAIRS):
                        nxt = ahead(b, q, w, w_next, k, AHEAD_RELU)
                        if nxt:
                            pair_relu(*nxt)
                        if k in MAX_AFTER and w_next and MAX_AFTER.index(k) < w_next // P:
                            rows_relu(b + 1, MAX_AFTER.index(k))
                        act.wait_ge(shift_ready, b * PAIRS + k + 1)
                        for j in range(2):
                            ins = act.activation(ring[:, k, j, 0:w], ring[:, k, j, 0:w], ACT.Exp,
                                                 bias=f20[:, 2 * k + j:2 * k + j + 1])
                        ins.then_inc(exp_ready, 1)
                        if k == NM_AFTER and w_next:
                            spread_copy(b + 1, 1 - q, w_next)

                def start():
                    for s in range(SUB):
                        rows_relu(0, s, s < 2)
                    for k in range(AHEAD_RELU):
                        pair_relu(0, 0, BLK, k, k < 2)
                    spread_copy(0, 0, BLK)

                passes(act, one, start)

            @block.vector
            def _(dve):
                def rows_max(b, s, first=False):
                    t = b * SUB + s
                    dve.wait_ge(row_relu, t + 1)
                    dve.scalar_tensor_tensor(rl[:, s % 2, 0:N], f2_all[:, 0:N], SLOPE, rl[:, s % 2, 0:N],
                                             ALU.mult, ALU.add).then_inc(row_sum, 1)
                    dve.wait_ge(row_sum, t + 1)
                    dve.wait_ge(rows_loaded[s % 2], (2 * b + s // 2 + 1) * 16)
                    dve.memset(pace_v[:, s:s + 1], 0.0)
                    dve.tensor_tensor_reduce(rl[:, s % 2, 0:N], rl[:, s % 2, 0:N], rows[:, s % 2, 0:N], 1.0, -3.0e38,
                                             ALU.add, ALU.max, mcol[:, s:s + 1]).then_inc(row_max, 1)
                    dve.wait_ge(row_max, t + 1)
                    if not first:
                        dve.wait_ge(m_spread, b)
                    dve.tensor_scalar(diag[:, s, :], ident[:, :], mcol[:, s:s + 1], -1.0, ALU.mult,
                                      ALU.mult).then_inc(diag_ready, 1)

                def pair_sum(b, q, w, k):
                    slot = (q * PAIRS + k) % 2
                    dve.wait_ge(relu_ready, b * PAIRS + k + 1)
                    dve.wait_ge(pair_loaded[k], (b + 1) * 16)
                    dve.tensor_tensor(ring[:, k, :, 0:w], ring[:, k, :, 0:w], rp[:, slot, :, 0:w],
                                      ALU.add).then_inc(sum_ready, 1)

                def finish(b, w):
                    for s in range(w // P):
                        t = b * SUB + s
                        dve.wait_ge(acc_full, t + 1)
                        dve.reciprocal(rs[:, s:s + 1], acc[:, s, DM:DM + 1]).then_inc(rs_ready, 1)
                        dve.wait_ge(rs_ready, t + 1)
                        xt = X[:, bass.ds(t, 1), :].rearrange("p o d -> p (o d)")
                        dve.scalar_tensor_tensor(xt, acc[:, s, 0:DM], rs[:, s:s + 1], xt, ALU.mult,
                                                 ALU.add).then_inc(acc_read, 1)

                def one(b, q, w, w_next):
                    for k in range(PAIRS):
                        nxt = ahead(b, q, w, w_next, k, AHEAD_SUM)
                        if nxt:
                            pair_sum(*nxt)
                        if k in MAX_AFTER and w_next and MAX_AFTER.index(k) < w_next // P:
                            rows_max(b + 1, MAX_AFTER.index(k))
                    finish(b, w)

                def start():
                    dve.sem_inc(acc_read, SUB)
                    for s in range(SUB):
                        rows_max(0, s, True)
                    for k in range(AHEAD_SUM):
                        pair_sum(0, 0, BLK, k)

                passes(dve, one, start)

            @block.gpsimd
            def _(pool):
                def pair_shift(b, q, w, k):
                    pool.wait_ge(sum_ready, b * PAIRS + k + 1)
                    if k == 0:
                        pool.wait_ge(nm_ready, b + 1)
                    pool.tensor_tensor(ring[:, k, :, 0:w], ring[:, k, :, 0:w],
                                       nm[:, q, 0:w].unsqueeze(1).broadcast_to([P, 2, w]),
                                       ALU.add).then_inc(shift_ready, 1)

                def one(b, q, w, w_next):
                    for k in range(PAIRS):
                        nxt = ahead(b, q, w, w_next, k, AHEAD_SHIFT)
                        if nxt:
                            pair_shift(*nxt)

                def start():
                    for k in range(AHEAD_SHIFT):
                        pair_shift(0, 0, BLK, k)

                passes(pool, one, start)

            @block.tensor
            def _(pe):
                def spread(b, w, first=False):
                    pe.wait_ge(diag_ready, b * SUB + w // P)
                    if not first:
                        pe.wait_ge(nm_ready, b)
                    for s in range(w // P):
                        ins = pe.matmul(psM[:, s * P:(s + 1) * P], ones[:, :], diag[:, s, :], start=True, stop=True)
                    ins.then_inc(m_spread, 1)

                def one(b, q, w, w_next):
                    for k in range(PAIRS):
                        pe.wait_ge(exp_ready, b * PAIRS + k + 1)
                        for j in range(2):
                            last = k == PAIRS - 1 and j == 1
                            r = LAST if last else P
                            for s in range(w // P):
                                if k + j == 0:
                                    pe.wait_ge(acc_read, b * SUB + s + 1)
                                ins = pe.matmul(acc[:, s, 0:DM + 1], ring[0:r, k, j, s * P:(s + 1) * P],
                                                h1[0:r, 2 * k + j, :], start=(k + j == 0), stop=last)
                                if last:
                                    ins.then_inc(acc_full, 1)
                        if k < PAIRS - 1:
                            ins.then_inc(pair_used, 1)
                        else:
                            pe.wait_ge(acc_full, b * SUB + w // P)
                            pe.sem_inc(pair_used, 1)
                        if k == BC_AFTER and w_next:
                            spread(b + 1, w_next)

                passes(pe, one, lambda: spread(0, BLK, True))


NH, NE, D = 4, 4, 64
DV = D + 1
NEG = -3.0e38
EPS2 = 1e-8


def stage_attention_prepare(nc, X, hn, sxT, v1, ident, hl_wT, hl_b, hl_bT, wv2):
    with ExitStack() as ctx:
        m = Mem(nc, ctx)
        xn = hn
        xt = m.sb("ap_xt", [P, DC, NP])
        w_sb = m.sb("ap_w", [P, DC, DM])
        b_sb = m.sb("ap_b", [P, DM])
        bT_sb = m.sb("ap_bT", [P, DC])
        wv_sb = m.sb("ap_wv", [P, DC, P])
        psT = m.ps("ap_psT", [P, 2, BLK])
        psX = m.ps("ap_psX", [P, 2, BLK])
        psN = m.ps("ap_psN", [P, 2, BLK])
        psV = m.ps("ap_psV", [P, 2, BLK])
        w_loaded = m.sem("ap_w_loaded")
        chain = m.sem("ap_chain")
        x_full = m.sem("ap_x_full")
        x_read = m.sem("ap_x_read")
        n_full = m.sem("ap_n_full")
        n_read = m.sem("ap_n_read")
        v_full = m.sem("ap_v_full")
        v_read = m.sem("ap_v_read")
        ones = m.sem("ap_ones")
        ln = LayerNorm(m, "ln3", X, xn, xt, ident, psT)
        cols = [(c, c0, w) for c in range(DC) for c0, w in blocks_of_tokens()]

        with nc.Block() as block:
            @block.sync
            def _(sp):
                sp.dma_start(w_sb[:, :, :], hl_wT.rearrange("(c p) o -> p c o", p=P)).then_inc(w_loaded, 16)
                sp.dma_start(b_sb[:, :], row_on_all(hl_b)).then_inc(w_loaded, 16)
                sp.dma_start(bT_sb[:, :], hl_bT).then_inc(w_loaded, 16)
                sp.dma_start(wv_sb[:, :, :], wv2.rearrange("c p o -> p c o")).then_inc(w_loaded, 16)

            @block.gpsimd
            def _(pool):
                pool.memset(v1[:, :, :, D:DV], 1.0).then_inc(ones, 1)

            @block.tensor
            def _(pe):
                pe.wait_ge(w_loaded, 64)
                ln.tensor(pe)
                pe.wait_ge(ln.xt_ready, 2 * (NB + 1))
                for n, (o, c0, w) in enumerate(cols):
                    if n >= 2:
                        pe.wait_ge(x_read, n - 1)
                    for c in range(DC):
                        ins = pe.matmul(psX[:, n % 2, 0:w], w_sb[:, c, o * P:(o + 1) * P], xt[:, c, c0:c0 + w],
                                        start=(c == 0), stop=(c == DC - 1))
                    ins.then_inc(x_full, 1)
                for t in range(NT):
                    if t >= 2:
                        pe.wait_ge(n_read, t - 1)
                    for c in range(DC):
                        ins = pe.matmul(psN[:, t % 2, 0:DM], xt[:, c, t * P:(t + 1) * P], w_sb[:, c, :],
                                        start=(c == 0), stop=(c == DC - 1))
                    ins.then_inc(n_full, 1)
                pe.wait_ge(x_read, len(cols))
                for t in range(NT):
                    if t >= 2:
                        pe.wait_ge(v_read, t - 1)
                    for c in range(DC):
                        ins = pe.matmul(psV[:, t % 2, c * P:(c + 1) * P], sxT[:, c, t * P:(t + 1) * P], wv_sb[:, c, :],
                                        start=True, stop=True)
                    ins.then_inc(v_full, 1)

            @block.vector
            def _(dve):
                ln.vector(dve, Linker(dve, chain))
                dve.wait_ge(w_loaded, 64)
                dve.wait_ge(ln.turned, 2 * (NB + 1))
                for t in range(NT):
                    dve.wait_ge(n_full, t + 1)
                    dve.tensor_tensor(hn[:, t, :], psN[:, t % 2, 0:DM], b_sb[:, :], ALU.add).then_inc(n_read, 1)
                for t in range(NT):
                    dve.wait_ge(v_full, t + 1)
                    dve.tensor_copy(v1[:, t, :, 0:D], psV[:, t % 2, 0:DM].rearrange("p (n d) -> p n d", d=D)).then_inc(v_read, 1)

            @block.scalar
            def _(act):
                ln.scalar(act)
                act.wait_ge(w_loaded, 64)
                for n, (o, c0, w) in enumerate(cols):
                    act.wait_ge(x_full, n + 1)
                    act.activation(sxT[:, o, c0:c0 + w], psX[:, n % 2, 0:w], ACT.Identity,
                                   bias=bT_sb[:, o:o + 1]).then_inc(x_read, 1)


def attention_plan():
    blocks = blocks_of_tokens()
    units = [(b, e) for b in range(NB + 1) for e in range(NE)]

    def groups(b):
        w = blocks[b][1]
        out, per = [], 2 * BLK // w
        full = list(range(b * SUB))
        for i in range(0, len(full), per):
            out.append([(t, 0, w, j * w) for j, t in enumerate(full[i:i + per])])
        diag = [(b * SUB + s, s * P, w - s * P) for s in range(w // P)]
        for i in range(0, len(diag), 2):
            pair = diag[i:i + 2]
            out.append([(t, off, ww, sum(x[2] for x in pair[:j])) for j, (t, off, ww) in enumerate(pair)])
        return out

    def chunks(b):
        return [(s, c, BLK if c < b else (s + 1) * P) for s in range(blocks[b][1] // P) for c in range(b + 1)]

    plan, n_x, n_g, n_p = [], [0], [0], [0]
    xi = {}

    def x_item(kind, i):
        xi[kind, i] = n_x[0]
        plan.append((kind, i, n_x[0]))
        n_x[0] += 1

    def p1(u, some):
        for s, c, w in some:
            plan.append(("p1", u, s, c, w, n_p[0]))
            n_p[0] += 1

    all_groups = [(u, g) for u, (b, e) in enumerate(units) for g in range(len(groups(b)))]
    number = {ug: i for i, ug in enumerate(all_groups)}

    def scores(u, g):
        plan.append(("s", u, groups(units[u][0])[g], number[u, g], g == 0))

    x_item("k", 0)
    for u in range(3):
        x_item("q", u)
    for u in range(2):
        p1(u, chunks(0))
        plan.append(("m", u))
    x_item("r", 0)
    scores(0, 0)
    for u, (b, e) in enumerate(units):
        if u + 3 < len(units):
            if (u + 3) % NE == 0:
                x_item("k", (u + 3) // NE)
            x_item("q", u + 3)
        todo = chunks(units[u + 2][0]) if u + 2 < len(units) else []
        gs = groups(b)
        for g in range(len(gs)):
            if number[u, g] + 1 < len(all_groups):
                scores(*all_groups[number[u, g] + 1])
            share = -(-len(todo) // (len(gs) - g))
            p1(u + 2, todo[:share])
            todo = todo[share:]
            plan.append(("pv", u, gs[g], number[u, g], g == 0, g == len(gs) - 1))
            if g == 0 and u + 1 < len(units):
                x_item("r", u + 1)
        if u + 2 < len(units):
            plan.append(("m", u + 2))
        plan.append(("o", u))
        if b >= 1:
            plan.append(("g", b - 1, e))
    for piece in range(NE):
        plan.append(("g", NB, piece))
    return plan, xi, dict(x=n_x[0], g=len(all_groups), p=n_p[0], u=len(units))


def stage_attention(nc, hn, sxT, v1, ident, wq2, wk2, gate_w, gate_b):
    plan, xi, per = attention_plan()
    blocks = blocks_of_tokens()
    units = [(b, e) for b in range(NB + 1) for e in range(NE)]
    SCALE = float(D) ** 0.5
    with ExitStack() as ctx:
        m = Mem(nc, ctx)
        wq_sb = m.sb("at_wq", [P, NE, P])
        wk_sb = m.sb("at_wk", [P, P])
        gw_sb = m.sb("at_gw", [P, NE, NE * D])
        gb_sb = m.sb("at_gb", [P, NH, NE])
        vn = m.sb("at_vn", [P, NT, DV])
        ka = m.sb("at_ka", [P, NP], F32R)
        kb = m.sb("at_kb", [P, NP], F32R)
        qa = m.sb("at_qa", [P, NE, BLK], F32R)
        qb = m.sb("at_qb", [P, NE, BLK], F32R)
        pt = m.sb("at_pt", [P, 3, 2 * BLK])
        identb = m.sb("at_identb", [P, P], BF16)
        hide_row = m.sb("at_hide_row", [P, P], BF16)
        hide_col = m.sb("at_hide_col", [P, P], BF16)
        mx = m.sb("at_mx", [P, 2, SUB, NB + 1])
        negm = m.sb("at_negm", [P, NE, SUB])
        o_sb = m.sb("at_o", [P, 2, NE, SUB, DV])
        on = m.sb("at_on", [P, SUB, NE, D])
        prod = m.sb("at_prod", [P, 2, SUB, NE * D])
        ro = m.sb("at_ro", [P, NE, SUB])
        pm = m.sb("at_pm", [P, SUB, D])
        gl = m.sb("at_gl", [P, SUB, NE])
        gm = m.sb("at_gm", [P, SUB])
        gs = m.sb("at_gs", [P, SUB, NE])
        mixed = m.sb("at_mixed", [P, SUB, D])
        psS = m.ps("at_psS", [P, 2, BLK])
        psP = m.ps("at_psP", [P, 2, 2 * BLK])
        psO = m.ps("at_psO", [P, BLK])
        psX = m.ps("at_psX", [P, BLK])
        consts = m.sem("at_consts")
        hides = m.sem("at_hides")
        gb_loaded = m.sem("at_gb_loaded")
        w_loaded = m.sem("at_w_loaded")
        v_ready = m.sem("at_v_ready")
        x_full, x_half, x_read = m.sem("at_x_full"), m.sem("at_x_half"), m.sem("at_x_read")
        p1_full, p1_read = m.sem("at_p1_full"), m.sem("at_p1_read")
        m_ready = m.sem("at_m_ready")
        s_full, e_ready, pv_done = m.sem("at_s_full"), m.sem("at_e_ready"), m.sem("at_pv_done")
        o_full, o_read = m.sem("at_o_full"), m.sem("at_o_read")
        on_ready, masked = m.sem("at_on_ready"), m.sem("at_masked")
        prod_ready, prod_read = m.sem("at_prod_ready"), m.sem("at_prod_read")
        gate_shifted, gate_exped, gate_ready = m.sem("at_gate_shifted"), m.sem("at_gate_exped"), m.sem("at_gate_ready")
        weighed, mix_done = m.sem("at_weighed"), m.sem("at_mix_done")
        chain = m.sem("at_chain")
        head_done = m.sem("at_head_done")
        NBLK = NB + 1
        n_q = per["u"] + NBLK

        def chunk_of(n):
            return n // 2

        def link_of(eng):
            return eng

        with nc.Block() as block:
            @block.sync
            def _(sp):
                sp.dma_start(gb_sb[:, :, :].rearrange("p n e -> p (n e)"), row_on_all(gate_b)).then_inc(gb_loaded, 16)
                with sp.Fori(0, NH) as n:
                    sp.wait_ge(head_done, n * 4)
                    sp.dma_start(wq_sb[:, :, :], wq2[bass.ds(n, 1), :, :, :].rearrange("o p e w -> p (o e) w")).then_inc(w_loaded, 16)
                    sp.dma_start(wk_sb[:, :], wk2[bass.ds(n, 1), :, :].rearrange("o p w -> p (o w)")).then_inc(w_loaded, 16)
                    sp.dma_start(gw_sb[:, :, :].rearrange("p e f -> p (e f)"),
                                 gate_w[bass.ds(n, 1), :].rearrange("o f -> (o f)").partition_broadcast(P)).then_inc(w_loaded, 16)

            @block.tensor
            def _(pe):
                pe.wait_ge(hides, 6)
                with pe.Fori(0, NH) as n:
                    pe.wait_ge(head_done, n * 4)
                    pe.wait_ge(w_loaded, n * 48 + 48)

                    def x_start(i):
                        if i > 0:
                            pe.wait_ge(x_read, n * per["x"] + i)

                    for step in plan:
                        kind = step[0]
                        if kind in ("k", "q"):
                            _, i, x = step
                            x_start(x)
                            c0, w = blocks[i if kind == "k" else units[i][0]]
                            lhs = wk_sb[:, :] if kind == "k" else wq_sb[:, units[i][1], :]
                            src = sxT[:, bass.ds(chunk_of(n), 1), c0:c0 + w].rearrange("p o w -> p (o w)")
                            pe.matmul(psX[:, 0:w], lhs, src, start=True, stop=True).then_inc(x_full, 1)
                        elif kind == "p1":
                            _, u, s, c, w, i = step
                            b, e = units[u]
                            pe.wait_ge(x_read, n * per["x"] + xi["q", u] + 1)
                            if i >= 2:
                                pe.wait_ge(p1_read, n * per["p"] + i - 1)
                            ins = pe.matmul(psS[:, i % 2, 0:w], qa[:, e, s * P:(s + 1) * P], ka[:, c * BLK:c * BLK + w],
                                            start=True, stop=(c < b))
                            if c == b:
                                ins = pe.matmul(psS[:, i % 2, s * P:(s + 1) * P], identb[:, :], hide_row[:, :],
                                                start=False, stop=True)
                            ins.then_inc(p1_full, 1)
                        elif kind == "r":
                            _, u, x = step
                            b, e = units[u]
                            x_start(x)
                            pe.wait_ge(m_ready, n * per["u"] + u + 1)
                            for s in range(blocks[b][1] // P):
                                ins = pe.transpose(psX[0:1, s * P:(s + 1) * P], negm[:, e, s:s + 1], ident[:, :])
                            ins.then_inc(x_full, 1)
                        elif kind == "s":
                            _, u, group, i, first = step
                            b, e = units[u]
                            if first:
                                pe.wait_ge(x_read, n * per["x"] + xi["r", u] + 1)
                            if i >= 2:
                                pe.wait_ge(e_ready, n * per["g"] + i - 1)
                            for t, off, w, at in group:
                                o = psP[:, i % 2, at:at + w]
                                diag = t >= b * SUB
                                pe.matmul(o, ka[:, t * P:(t + 1) * P], qa[:, e, off:off + w], start=True, stop=False)
                                ins = pe.matmul(o, kb[:, t * P:(t + 1) * P], qb[:, e, off:off + w], start=False, stop=not diag)
                                if diag:
                                    ins = pe.matmul(psP[:, i % 2, at:at + P], identb[:, :], hide_col[:, :],
                                                    start=False, stop=True)
                            ins.then_inc(s_full, 1)
                        elif kind == "pv":
                            _, u, group, i, first, last = step
                            b, e = units[u]
                            ws = blocks[b][1] // P
                            if first and u > 0:
                                pe.wait_ge(o_read, n * per["u"] + u)
                            if first and u == 0:
                                pe.wait_ge(v_ready, n + 1)
                            pe.wait_ge(e_ready, n * per["g"] + i + 1)
                            for t, off, w, at in group:
                                for s in range(off // P, ws):
                                    ins = pe.matmul(psO[:, s * DV:(s + 1) * DV],
                                                    pt[:, i % 3, at + s * P - off:at + (s + 1) * P - off], vn[:, t, :],
                                                    start=(t == 0 and s == 0), stop=(t == b * SUB + s),
                                                    skip_group_check=True)
                            ins.then_inc(pv_done, 1)
                            if last:
                                pe.wait_ge(pv_done, n * per["g"] + i + 1)
                                pe.sem_inc(o_full, 1)
                    pe.sem_inc(head_done, 1)

            @block.scalar
            def _(act):
                act.wait_ge(consts, 4)
                with act.Fori(0, NH) as n:
                    act.wait_ge(head_done, n * 4)
                    for step in plan:
                        kind = step[0]
                        if kind == "k":
                            _, c, x = step
                            c0, w = blocks[c]
                            act.wait_ge(x_full, n * per["x"] + x + 1)
                            act.activation(ka[0:D, c0:c0 + w], psX[0:D, 0:w], ACT.Copy)
                            act.activation(kb[D:P, c0:c0 + w], psX[D:P, 0:w], ACT.Copy).then_inc(x_half, 1)
                        elif kind == "q":
                            _, u, x = step
                            b, e = units[u]
                            w = blocks[b][1]
                            act.wait_ge(x_full, n * per["x"] + x + 1)
                            act.activation(qa[:, e, 0:w], psX[:, 0:w], ACT.Copy, scale=SCALE).then_inc(x_half, 1)
                        elif kind == "r":
                            _, u, x = step
                            b, e = units[u]
                            w = blocks[b][1]
                            act.wait_ge(x_full, n * per["x"] + x + 1)
                            act.activation(qb[0:1, e, 0:w], psX[0:1, 0:w], ACT.Copy).then_inc(x_read, 1)
                        elif kind == "s":
                            _, u, group, i, first = step
                            w = sum(x[2] for x in group)
                            act.wait_ge(s_full, n * per["g"] + i + 1)
                            if i >= 3:
                                act.wait_ge(pv_done, n * per["g"] + i - 2)
                            act.activation(pt[:, i % 3, 0:w], psP[:, i % 2, 0:w], ACT.Exp).then_inc(e_ready, 1)
                        elif kind == "g" and step[2] == 3:
                            b = step[1]
                            ws = blocks[b][1] // P
                            act.wait_ge(gate_shifted, n * NBLK + b + 1)
                            act.activation(gs[:, 0:ws, :], gl[:, 0:ws, :], ACT.Exp).then_inc(gate_exped, 1)
                    act.wait_ge(gate_exped, n * NBLK + NBLK)
                    act.sem_inc(head_done, 1)

            @block.vector
            def _(dve):
                dve.wait_ge(gb_loaded, 16)
                dve.wait_ge(consts, 4)
                with dve.Fori(0, NH) as n:
                    dve.wait_ge(head_done, n * 4)
                    dve.wait_ge(w_loaded, n * 48 + 48)
                    seen = [0, 0]
                    LINKS = NBLK * 6

                    def link(ins):
                        ins.then_inc(chain, 1)
                        seen[0] += 1
                        dve.wait_ge(chain, n * LINKS + seen[0])

                    for step in plan:
                        kind = step[0]
                        if kind == "k":
                            _, c, x = step
                            c0, w = blocks[c]
                            seen[1] += 1
                            dve.wait_ge(x_half, n * n_q + seen[1])
                            dve.tensor_tensor(ka[D:P, c0:c0 + w], psX[D:P, 0:w], kb[D:P, c0:c0 + w].bitcast(F32),
                                              ALU.subtract).then_inc(x_read, 1)
                        elif kind == "q":
                            _, u, x = step
                            b, e = units[u]
                            w = blocks[b][1]
                            seen[1] += 1
                            dve.wait_ge(x_half, n * n_q + seen[1])
                            dve.scalar_tensor_tensor(qb[D:P, e, 0:w], psX[D:P, 0:w], SCALE, qa[D:P, e, 0:w].bitcast(F32),
                                                     ALU.mult, ALU.subtract).then_inc(x_read, 1)
                        elif kind == "p1":
                            _, u, s, c, w, i = step
                            dve.wait_ge(p1_full, n * per["p"] + i + 1)
                            dve.tensor_reduce(mx[:, u % 2, s, c:c + 1], psS[:, i % 2, 0:w], AX.X, ALU.max).then_inc(p1_read, 1)
                            if s == blocks[units[u][0]][1] // P - 1 and c == units[u][0]:
                                dve.wait_ge(p1_read, n * per["p"] + i + 1)
                        elif kind == "m":
                            _, u = step
                            b, e = units[u]
                            ws = blocks[b][1] // P
                            dve.tensor_reduce(negm[:, e, 0:ws], mx[:, u % 2, 0:ws, 0:b + 1], AX.X, ALU.max,
                                              negate=True).then_inc(m_ready, 1)
                        elif kind == "o":
                            _, u = step
                            b, e = units[u]
                            ws = blocks[b][1] // P
                            dve.wait_ge(o_full, n * per["u"] + u + 1)
                            dve.tensor_copy(o_sb[:, b % 2, e, 0:ws, :],
                                            psO[:, 0:ws * DV].rearrange("p (s d) -> p s d", d=DV)).then_inc(o_read, 1)
                        elif kind == "g":
                            _, b, piece = step
                            ws = blocks[b][1] // P
                            hsl = hn[:, b * SUB:b * SUB + ws, bass.ds(n * D, D)]
                            if piece == 0:
                                dve.wait_ge(o_read, n * per["u"] + b * NE + NE)
                                link(dve.reciprocal(ro[:, :, 0:ws], o_sb[:, b % 2, :, 0:ws, D]))
                                for e in range(NE):
                                    ins = dve.tensor_tensor(on[:, 0:ws, e, :], o_sb[:, b % 2, e, 0:ws, 0:D],
                                                            ro[:, e, 0:ws].unsqueeze(2).broadcast_to([P, ws, D]), ALU.mult)
                                dve.tensor_scalar(pm[:, 0:ws, :], hsl, 0.0, None, ALU.not_equal).then_inc(on_ready, 1)
                            elif piece in (1, 2):
                                for g in (2 * piece - 2, 2 * piece - 1):
                                    dve.wait_ge(prod_ready, n * NBLK * NE + b * NE + g + 1)
                                    dve.tensor_reduce(gl[:, 0:ws, g:g + 1], prod[:, g % 2, 0:ws, :], AX.X,
                                                      ALU.add).then_inc(prod_read, 1)
                                if piece == 2:
                                    dve.wait_ge(prod_read, n * NBLK * NE + b * NE + NE)
                                    link(dve.tensor_tensor(gl[:, 0:ws, :], gl[:, 0:ws, :],
                                                           gb_sb[:, bass.ds(n, 1), :].broadcast_to([P, ws, NE]), ALU.add))
                                    link(dve.tensor_reduce(gm[:, 0:ws], gl[:, 0:ws, :], AX.X, ALU.max))
                                    dve.tensor_tensor(gl[:, 0:ws, :], gl[:, 0:ws, :],
                                                      gm[:, 0:ws].unsqueeze(2).broadcast_to([P, ws, NE]),
                                                      ALU.subtract).then_inc(gate_shifted, 1)
                            else:
                                dve.wait_ge(gate_exped, n * NBLK + b + 1)
                                link(dve.tensor_reduce(gm[:, 0:ws], gs[:, 0:ws, :], AX.X, ALU.add))
                                link(dve.reciprocal(gm[:, 0:ws], gm[:, 0:ws]))
                                dve.tensor_tensor(gs[:, 0:ws, :], gs[:, 0:ws, :],
                                                  gm[:, 0:ws].unsqueeze(2).broadcast_to([P, ws, NE]),
                                                  ALU.mult).then_inc(gate_ready, 1)
                                dve.wait_ge(weighed, n * NBLK + b + 1)
                                link(dve.tensor_reduce(mixed[:, 0:ws, :], on[:, 0:ws, :, :].rearrange("p s e d -> p s d e"),
                                                       AX.X, ALU.add))
                                dve.tensor_tensor(hsl, hsl, mixed[:, 0:ws, :], ALU.add).then_inc(mix_done, 1)
                    LINKS_USED = seen[0]
                    assert LINKS_USED == LINKS, (LINKS_USED, LINKS)
                    dve.wait_ge(mix_done, n * NBLK + NBLK)
                    dve.sem_inc(head_done, 1)

            @block.gpsimd
            def _(pool):
                pool.memset(kb[0:D, :].bitcast(F32), 0.0).then_inc(consts, 1)
                pool.memset(qb[0:D, :, :].bitcast(F32), 0.0).then_inc(consts, 1)
                pool.wait_ge(consts, 2)
                pool.memset(kb[0:1, :].bitcast(F32), 1.0).then_inc(consts, 1)
                pool.memset(mx[:, :, :, :], 0.0).then_inc(consts, 1)
                pool.memset(identb[:, :], 0.0).then_inc(hides, 1)
                pool.memset(hide_row[:, :], 0.0).then_inc(hides, 1)
                pool.memset(hide_col[:, :], 0.0).then_inc(hides, 1)
                pool.wait_ge(hides, 3)
                pool.wait_ge(consts, 4)
                pool.affine_select(out=identb[:, :], in_=identb[:, :], compare_op=ALU.not_equal, fill=1.0, base=0,
                                   pattern=[[-1, P]], channel_multiplier=1).then_inc(hides, 1)
                pool.affine_select(out=hide_row[:, :], in_=hide_row[:, :], compare_op=ALU.is_ge, fill=NEG, base=0,
                                   pattern=[[-1, P]], channel_multiplier=1).then_inc(hides, 1)
                pool.affine_select(out=hide_col[:, :], in_=hide_col[:, :], compare_op=ALU.is_ge, fill=NEG, base=0,
                                   pattern=[[1, P]], channel_multiplier=-1).then_inc(hides, 1)
                with pool.Fori(0, NH) as n:
                    pool.wait_ge(head_done, n * 4)
                    pool.wait_ge(w_loaded, n * 48 + 48)
                    pool.tensor_copy(vn[:, :, :], v1[:, :, bass.ds(n, 1), :].rearrange("p t o d -> p t (o d)")).then_inc(v_ready, 1)
                    for b in range(NBLK):
                        ws = blocks[b][1] // P
                        pool.wait_ge(on_ready, n * NBLK + b + 1)
                        pool.tensor_tensor(on[:, 0:ws, :, :], on[:, 0:ws, :, :],
                                           pm[:, 0:ws, :].unsqueeze(2).broadcast_to([P, ws, NE, D]),
                                           ALU.mult).then_inc(masked, 1)
                        pool.wait_ge(masked, n * NBLK + b + 1)
                        for g in range(NE):
                            if g >= 2:
                                pool.wait_ge(prod_read, n * NBLK * NE + b * NE + g - 1)
                            pool.tensor_tensor(prod[:, g % 2, 0:ws, :], on[:, 0:ws, :, :].rearrange("p s e d -> p s (e d)"),
                                               gw_sb[:, g:g + 1, :].broadcast_to([P, ws, NE * D]),
                                               ALU.mult).then_inc(prod_ready, 1)
                        pool.wait_ge(gate_ready, n * NBLK + b + 1)
                        pool.wait_ge(prod_ready, n * NBLK * NE + b * NE + NE)
                        pool.tensor_tensor(on[:, 0:ws, :, :], on[:, 0:ws, :, :],
                                           gs[:, 0:ws, :].unsqueeze(3).broadcast_to([P, ws, NE, D]),
                                           ALU.mult).then_inc(weighed, 1)
                    pool.wait_ge(weighed, n * NBLK + NBLK)
                    pool.sem_inc(head_done, 1)


def stage_ffn(nc, X, hn, ident, io, out):
    blocks = blocks_of_tokens()
    NBLK = len(blocks)
    with ExitStack() as ctx:
        m = Mem(nc, ctx)
        fc1 = m.sb("ff_fc1", [P, P])
        fc2 = m.sb("ff_fc2", [P, P])
        b1 = m.sb("ff_b1", [P, 1])
        b2 = m.sb("ff_b2", [P, D])
        lng = m.sb("ff_lng", [P, D])
        lnb = m.sb("ff_lnb", [P, D])
        fng = m.sb("ff_fng", [P, D])
        fnb = m.sb("ff_fnb", [P, D])
        fgw = m.sb("ff_fgw", [P, DC, NH])
        stats = m.sb("ff_stats", [P, 2, SUB * NH, 6])
        mv = m.sb("ff_mv", [P, 2, SUB * NH, 2])
        var = m.sb("ff_var", [P, 2, SUB * NH])
        std = m.sb("ff_std", [P, 2, SUB * NH])
        fxT = m.sb("ff_fxT", [P, DC, BLK])
        h1T = m.sb("ff_h1T", [P, DC, BLK])
        y = m.sb("ff_y", [P, 2, SUB, NH, D])
        foT = m.sb("ff_foT", [P, DC, BLK])
        gl = m.sb("ff_gl", [P, SUB, NH])
        gm = m.sb("ff_gm", [P, SUB])
        ge = m.sb("ff_ge", [P, SUB, NH])
        psT = m.ps("ff_psT", [P, DC, BLK])
        psF = m.ps("ff_psF", [P, DC, BLK])
        ps2 = m.ps("ff_ps2", [P, SUB, DM])
        psG = m.ps("ff_psG", [P, BLK])
        w_loaded = m.sem("ff_w_loaded")
        chain = m.sem("ff_chain")
        var_ready, std_ready = m.sem("ff_var_ready"), m.sem("ff_std_ready")
        normed, scaled, affine = m.sem("ff_normed"), m.sem("ff_scaled"), m.sem("ff_affine")
        t_full, t_read = m.sem("ff_t_full"), m.sem("ff_t_read")
        f_full, h1_ready, h1_masked = m.sem("ff_f_full"), m.sem("ff_h1_ready"), m.sem("ff_h1_masked")
        p2_full, p2_read = m.sem("ff_p2_full"), m.sem("ff_p2_read")
        g_full, g_shifted, g_exped = m.sem("ff_g_full"), m.sem("ff_g_shifted"), m.sem("ff_g_exped")
        x_done = m.sem("ff_x_done")
        stored = m.sem("ff_stored")

        def tiles(b):
            c0, w = blocks[b]
            return c0 // P, w // P

        def fx_of(b):
            t0, ws = tiles(b)
            return hn[:, t0:t0 + ws, :].rearrange("p t (n d) -> p (t n) d", d=D)

        def y_of(b):
            _, ws = tiles(b)
            return y[:, b % 2, 0:ws, :, :].rearrange("p t n d -> p (t n) d")

        order = [(0, 0)]
        for b in range(NBLK):
            if b + 1 < NBLK:
                order.append((b + 1, 0))
            order.append((b, 1))
        at = {x: i for i, x in enumerate(order)}

        with nc.Block() as block:
            @block.sync
            def _(sp):
                for dst, src in ((fc1[:, :], io["fc1"]), (fc2[:, :], io["fc2"]), (b1[:, :], io["fc1_b"]),
                                 (b2[:, :], row_on_all(io["fc2_b"])), (lng[:, :], row_on_all(io["ln_g"])),
                                 (lnb[:, :], row_on_all(io["ln_b"])), (fng[:, :], row_on_all(io["fnorm_g"])),
                                 (fnb[:, :], row_on_all(io["fnorm_b"])),
                                 (fgw[:, :, :], io["fgate"].rearrange("(c p) n -> p c n", p=P))):
                    sp.dma_start(dst, src).then_inc(w_loaded, 16)
                for b in range(NBLK):
                    t0, ws = tiles(b)
                    sp.wait_ge(x_done, b + 1)
                    if b < NBLK - 1:
                        sp.dma_start(out[t0 * P:(t0 + ws) * P, :].rearrange("(t p) d -> p t d", p=P),
                                     X[:, t0:t0 + ws, :]).then_inc(stored, 16)
                    else:
                        sp.dma_start(out[t0 * P:(NT - 1) * P, :].rearrange("(t p) d -> p t d", p=P),
                                     X[:, t0:NT - 1, :]).then_inc(stored, 16)
                        sp.dma_start(out[(NT - 1) * P:N, :], X[0:LAST, NT - 1, :]).then_inc(stored, 16)
                sp.wait_ge(stored, 16 * (NBLK + 1))

            @block.vector
            def _(dve):
                link = Linker(dve, chain)
                dve.wait_ge(w_loaded, 9 * 16)

                def norm(b, which, v):
                    i = at[b, which]
                    groups = tiles(b)[1] * NH
                    for g in range(groups):
                        ins = dve.bn_stats(stats[:, which, g, :], v[:, g, :])
                    link(ins)
                    for g in range(groups):
                        ins = dve.bn_aggr(mv[:, which, g, :], stats[:, which, g, :])
                    link(ins)
                    dve.tensor_scalar(var[:, which, 0:groups], mv[:, which, 0:groups, 1], EPS2, None,
                                      ALU.add).then_inc(var_ready, 1)
                    dve.wait_ge(std_ready, i + 1)
                    link(dve.reciprocal(std[:, which, 0:groups], std[:, which, 0:groups]))
                    for g in range(groups):
                        ins = dve.tensor_scalar(v[:, g, :], v[:, g, :], mv[:, which, g, 0:1], std[:, which, g:g + 1],
                                                ALU.subtract, ALU.mult)
                    ins.then_inc(normed, 1)

                def mask_hidden(b):
                    w = blocks[b][1]
                    dve.wait_ge(h1_ready, b + 1)
                    dve.scalar_tensor_tensor(h1T[:, :, 0:w], fxT[:, :, 0:w], 0.0, h1T[:, :, 0:w], ALU.not_equal,
                                             ALU.mult).then_inc(h1_masked, 1)

                def second(b):
                    ws = tiles(b)[1]
                    dve.wait_ge(p2_full, b + 1)
                    yv = y_of(b)
                    dve.tensor_tensor(yv, ps2[:, 0:ws, :].rearrange("p t (n d) -> p (t n) d", d=D),
                                      b2[:, :].unsqueeze(1).broadcast_to([P, ws * NH, D]), ALU.add).then_inc(p2_read, 1)
                    dve.wait_ge(p2_read, b + 1)
                    link(dve.scalar_tensor_tensor(yv, fx_of(b), 0.0, yv, ALU.not_equal, ALU.mult))
                    link(dve.tensor_tensor(yv, yv, fx_of(b), ALU.add))
                    norm(b, 1, yv)

                def gate(b):
                    t0, ws = tiles(b)
                    dve.wait_ge(g_full, b + 1)
                    g3 = psG[:, 0:ws * NH].rearrange("p (t n) -> p t n", n=NH)
                    link(dve.tensor_reduce(gm[:, 0:ws], g3, AX.X, ALU.max))
                    dve.tensor_tensor(gl[:, 0:ws, :], g3, gm[:, 0:ws].unsqueeze(2).broadcast_to([P, ws, NH]),
                                      ALU.subtract).then_inc(g_shifted, 1)
                    dve.wait_ge(g_exped, b + 1)
                    link(dve.tensor_reduce(gm[:, 0:ws], ge[:, 0:ws, :], AX.X, ALU.add))
                    link(dve.reciprocal(gm[:, 0:ws], gm[:, 0:ws]))
                    link(dve.tensor_tensor(gl[:, 0:ws, :], ge[:, 0:ws, :], gm[:, 0:ws].unsqueeze(2).broadcast_to([P, ws, NH]),
                                           ALU.mult))
                    yv = y_of(b)
                    link(dve.tensor_tensor(yv, yv, gl[:, 0:ws, :].rearrange("p t n -> p (t n)").unsqueeze(2)
                                           .broadcast_to([P, ws * NH, D]), ALU.mult))
                    dve.tensor_tensor(X[:, t0:t0 + ws, :], X[:, t0:t0 + ws, :],
                                      y[:, b % 2, 0:ws, :, :].rearrange("p t n d -> p t (n d)"), ALU.add).then_inc(x_done, 1)

                for b in range(NBLK + 1):
                    if b < NBLK:
                        norm(b, 0, fx_of(b))
                    if b >= 1:
                        second(b - 1)
                    if b < NBLK:
                        mask_hidden(b)
                    if b >= 1:
                        gate(b - 1)

            @block.gpsimd
            def _(pool):
                pool.wait_ge(w_loaded, 9 * 16)
                for i, (b, which) in enumerate(order):
                    v = (fx_of, y_of)[which](b)
                    groups = tiles(b)[1] * NH
                    scale, offset = ((lng, lnb), (fng, fnb))[which]
                    pool.wait_ge(normed, i + 1)
                    pool.tensor_tensor(v, v, scale[:, :].unsqueeze(1).broadcast_to([P, groups, D]),
                                       ALU.mult).then_inc(scaled, 1)
                    pool.wait_ge(scaled, i + 1)
                    pool.tensor_tensor(v, v, offset[:, :].unsqueeze(1).broadcast_to([P, groups, D]),
                                       ALU.add).then_inc(affine, 1)

            @block.scalar
            def _(act):
                n_turn = 0

                def root(b, which):
                    act.wait_ge(var_ready, at[b, which] + 1)
                    act.activation(std[:, which, :], var[:, which, :], ACT.Sqrt).then_inc(std_ready, 1)

                def copy_turned(b, dst):
                    nonlocal n_turn
                    n_turn += 1
                    w = blocks[b][1]
                    act.wait_ge(t_full, n_turn)
                    act.activation(dst[:, :, 0:w], psT[:, :, 0:w], ACT.Copy).then_inc(t_read, 1)

                act.wait_ge(w_loaded, 9 * 16)
                for b in range(NBLK + 1):
                    if b < NBLK:
                        w = blocks[b][1]
                        root(b, 0)
                        copy_turned(b, fxT)
                        act.wait_ge(f_full, b + 1)
                        act.activation(h1T[:, :, 0:w], psF[:, :, 0:w], ACT.Relu, bias=b1[:, 0:1]).then_inc(h1_ready, 1)
                    if b >= 1:
                        root(b - 1, 1)
                        copy_turned(b - 1, foT)
                        act.wait_ge(g_shifted, b)
                        ws = tiles(b - 1)[1]
                        act.activation(ge[:, 0:ws, :], gl[:, 0:ws, :], ACT.Exp).then_inc(g_exped, 1)

            @block.tensor
            def _(pe):
                n_turn = 0

                def turn(b, which):
                    nonlocal n_turn
                    t0, ws = tiles(b)
                    pe.wait_ge(affine, at[b, which] + 1)
                    if n_turn:
                        pe.wait_ge(t_read, n_turn)
                    n_turn += 1
                    for c in range(DC):
                        for s in range(ws):
                            src = hn[:, t0 + s, c * P:(c + 1) * P] if which == 0 else \
                                y[:, b % 2, s, 2 * c:2 * c + 2, :].rearrange("p n d -> p (n d)")
                            ins = pe.transpose(psT[:, c, s * P:(s + 1) * P], src, ident[:, :])
                    ins.then_inc(t_full, 1)

                pe.wait_ge(w_loaded, 9 * 16)
                for b in range(NBLK + 1):
                    if b < NBLK:
                        w = blocks[b][1]
                        turn(b, 0)
                        pe.wait_ge(t_read, n_turn)
                        if b >= 1:
                            pe.wait_ge(h1_ready, b)
                        for c in range(DC):
                            ins = pe.matmul(psF[:, c, 0:w], fc1[:, :], fxT[:, c, 0:w], start=True, stop=True)
                        ins.then_inc(f_full, 1)
                    if b >= 1:
                        turn(b - 1, 1)
                        pe.wait_ge(t_read, n_turn)
                        if b >= 2:
                            pe.wait_ge(g_shifted, b - 1)
                        for s in range(tiles(b - 1)[1]):
                            for c in range(DC):
                                ins = pe.matmul(psG[:, s * NH:(s + 1) * NH], foT[:, c, s * P:(s + 1) * P], fgw[:, c, :],
                                                start=(c == 0), stop=(c == DC - 1))
                        ins.then_inc(g_full, 1)
                    if b < NBLK:
                        pe.wait_ge(h1_masked, b + 1)
                        if b >= 1:
                            pe.wait_ge(p2_read, b)
                        for s in range(tiles(b)[1]):
                            for c in range(DC):
                                ins = pe.matmul(ps2[:, s, c * P:(c + 1) * P], h1T[:, c, s * P:(s + 1) * P], fc2[:, :],
                                                start=True, stop=True)
                        ins.then_inc(p2_full, 1)


def two_layers(nc, io, out):
    with ExitStack() as ctx:
        m = Mem(nc, ctx)
        X = m.sb("X", [P, NT, DM])
        ident = m.sb("ident", [P, P])
        with ExitStack() as layer0:
            m0 = Mem(nc, layer0)
            xn = m0.sb("xn", [P, NT, DM])
            dinv = m0.sb("dinv", [P, NT])
            stage_degrees(nc, X, xn, dinv, ident, io["x"], io["adj"])
            stage_gcn(nc, X, xn, dinv, io["adjT"], io["gcn_wT"], io["gcn_b"])
        with ExitStack() as slices:
            ms = Mem(nc, slices)
            swT = ms.sb("swT", [P, KC, NP])
            tok = ms.sb("tok", [P, KC, DM + 1])
            stage_slices(nc, X, swT, tok, ident, io["w_x"], io["w_sliceT"], io["b_x"], io["b_slice"], io["temp"])
            stage_hydra(nc, X, swT, tok, ident, io)
        with ExitStack() as gat:
            mg = Mem(nc, gat)
            h1 = mg.sb("h1", [P, NT, DM + 1])
            f1_all = mg.sb("f1_all", [P, NP])
            f2_all = mg.sb("f2_all", [P, NP])
            f18, f28, f20 = mg.sb("f18", [P, NT]), mg.sb("f28", [P, NT]), mg.sb("f20", [P, NT])
            ones = mg.sb("ones", [P, P])
            stage_gat_prepare(nc, X, h1, f1_all, f2_all, f18, f28, f20, ident, ones, io["gat_w"], io["gat_wT"],
                              io["gat_conv"], io["gat_b"])
            stage_gat(nc, X, h1, f1_all, f2_all, f18, f28, f20, ident, ones, io["adj"], io["adjT"])
        hn = m.sb("hn", [P, NT, DM])
        with ExitStack() as attention:
            ma = Mem(nc, attention)
            sxT = ma.sb("sxT", [P, DC, NP])
            v1 = ma.sb("v1", [P, NT, NH, DV])
            stage_attention_prepare(nc, X, hn, sxT, v1, ident, io["hl_wT"], io["hl_b"], io["hl_bT"], io["wv2"])
            stage_attention(nc, hn, sxT, v1, ident, io["wq2"], io["wk2"], io["gate_w"], io["gate_b"])
        stage_ffn(nc, X, hn, ident, io, out)


def on_diagonal(w, n):
    k, o = w.shape[1], w.shape[0]
    z = np.zeros((n * k, n * o), w.dtype)
    for i in range(n):
        z[i * k:(i + 1) * k, i * o:(i + 1) * o] = w.T
    return z


def laid_out(a):
    pad = NP - N
    l0, f0, g1, f1 = "L0_gnn_", "L0_ffn_", "L1_gnn_", "L1_ffn_"
    adj = a["adj"]
    wq2 = np.zeros((NH, P, NE, P), np.float32)
    wk2 = np.zeros((NH, P, P), np.float32)
    wv2 = np.zeros((DC, P, P), np.float32)
    for n in range(NH):
        r = (n % 2) * D
        wk2[n, r:r + D, 0:D] = wk2[n, r:r + D, D:P] = a[f1 + "wk"][n].T
        wv2[n // 2, r:r + D, r:r + D] = a[f1 + "wv"][n].T
        for e in range(NE):
            wq2[n, r:r + D, e, 0:D] = wq2[n, r:r + D, e, D:P] = a[f1 + "wq"][n, e].T
    hl_b = a[f1 + "hl_b"].reshape(-1)
    return {
        "x": a["x"],
        "adj": np.pad(adj, ((0, pad), (0, pad))),
        "adjT": np.pad(adj.T, ((0, pad), (0, pad))),
        "gcn_wT": a[l0 + "W"].T, "gcn_b": a[l0 + "b"],
        "w_x": a[f0 + "W_x"], "w_sliceT": a[f0 + "W_slice"].T, "b_x": a[f0 + "b_x"].reshape(H, PH).T,
        "b_slice": a[f0 + "b_slice"], "temp": a[f0 + "temperature"].reshape(H),
        "w_fxT": a[f0 + "W_fx"].T, "b_fx": a[f0 + "b_fx"], "in_wT": a[f0 + "hy_in_w"].T,
        "conv_w": a[f0 + "hy_conv_w"], "conv_b": by_group(a[f0 + "hy_conv_b"]), "dt_bias": a[f0 + "hy_dt_bias"],
        "A_log": a[f0 + "hy_A_log"], "D": a[f0 + "hy_D"], "fcD_wT": a[f0 + "hy_fcD_w"].T,
        "norm_w": a[f0 + "hy_norm_w"].reshape(XC, P).T, "hy_outT": a[f0 + "hy_out_w"].T,
        "out_wT": a[f0 + "out_w"].T, "out_b": a[f0 + "out_b"],
        "gat_w": a[g1 + "weight"], "gat_wT": a[g1 + "weight"].T,
        "gat_conv": np.concatenate([a[g1 + "conv_weight1"], a[g1 + "conv_weight2"]], axis=1), "gat_b": a[g1 + "bias"],
        "hl_wT": a[f1 + "hl_w"].reshape(NH * D, DM).T, "hl_b": hl_b, "hl_bT": hl_b.reshape(DC, P).T,
        "wq2": wq2, "wk2": wk2, "wv2": wv2,
        "gate_w": a[f1 + "gate_w"].reshape(NH, NE * NE * D), "gate_b": a[f1 + "gate_b"].reshape(NH * NE),
        "ln_g": a[f1 + "ln_g"], "ln_b": a[f1 + "ln_b"], "fnorm_g": a[f1 + "fnorm_g"], "fnorm_b": a[f1 + "fnorm_b"],
        "fc1": on_diagonal(a[f1 + "fc1_w"], 2), "fc2": on_diagonal(a[f1 + "fc2_w"], 2),
        "fc1_b": np.tile(a[f1 + "fc1_b"], 2)[:, None], "fc2_b": a[f1 + "fc2_b"],
        "fgate": a[f1 + "fgate_w"].T,
    }


def kernel(**inputs):
    import concourse.bacc as bacc
    from concourse.bass_utils import run_bass_kernel_spmd

    nc = bacc.Bacc("TRN2", target_bir_lowering=False, num_devices=1)
    arrays, io = {}, {}
    for name, a in laid_out({k: np.asarray(v) for k, v in inputs.items()}).items():
        arrays[f"in_{name}"] = np.ascontiguousarray(a)
        io[name] = nc.dram_tensor(f"in_{name}", a.shape, mybir.dt.from_np(a.dtype), kind="ExternalInput").ap()
    out = nc.dram_tensor("out_x", (N, DM), F32, kind="ExternalOutput").ap()
    two_layers(nc, io, out)
    r = run_bass_kernel_spmd(nc, [arrays], core_ids=[0])
    return r.results[0]["out_x"]
```
